# Optimizing a Trainium2 kernel written in Bass

```python
import numpy as np
import jax
import jax.numpy as jnp

def _softmax(x, axis=-1):
    return jax.nn.softmax(x, axis=axis)

def _gelu(x):
    return jax.nn.gelu(x, approximate=True)

def _silu(x):
    return jax.nn.silu(x)

def _sigmoid(x):
    return jax.nn.sigmoid(x)

def _layernorm(x, axis=-1, eps=1e-05):
    m = jnp.mean(x, axis=axis, keepdims=True)
    v = jnp.var(x, axis=axis, keepdims=True)
    return (x - m) / jnp.sqrt(v + eps)

def _scatter_add(tgt, idx, src, axis=0):
    return tgt.at[idx].add(src)

def _segment_sum(src, seg, n):
    return jax.ops.segment_sum(src, seg, n)
kernel_name = 'mk_adaln_d1_jaxref_r8_78a280'

def setup_inputs(seed: int=0):
    np.random.seed(seed)
    _w = jnp.asarray

    def _L0_attn_setup():
        import jax, jax.numpy as jnp
        import numpy as np
        B, T, C = (8, 512, 128)

        def _wkv(w_decay, u_first, k, v):
            w = -jnp.exp(w_decay)
            u = u_first
            kt = jnp.transpose(k, (1, 0, 2))
            vt = jnp.transpose(v, (1, 0, 2))
            a0 = jnp.zeros((k.shape[0], k.shape[2]), dtype=k.dtype)
            b0 = jnp.zeros_like(a0)
            p0 = jnp.full_like(a0, -1e+38)

            def step(carry, kv):
                a, b, p = carry
                k_t, v_t = kv
                q = jnp.maximum(p, u + k_t)
                e1 = jnp.exp(p - q)
                e2 = jnp.exp(u + k_t - q)
                y = (e1 * a + e2 * v_t) / (e1 * b + e2)
                q2 = jnp.maximum(p + w, k_t)
                f1 = jnp.exp(p + w - q2)
                f2 = jnp.exp(k_t - q2)
                return ((f1 * a + f2 * v_t, f1 * b + f2, q2), y)
            _, y = jax.lax.scan(step, (a0, b0, p0), (kt, vt))
            return jnp.transpose(y, (1, 0, 2))
        key = jax.random.key(seed)
        ks = jax.random.split(key, 5)
        scales = (jnp.arange(C, dtype=jnp.float32) / C).reshape(1, 1, C)
        return {'x': jax.random.normal(ks[0], (B, T, C), dtype=jnp.float32), 'time_decay': scales, 'time_first': scales, 'time_mix_k': scales, 'time_mix_v': scales, 'time_mix_r': scales, 'Wk': jax.random.normal(ks[1], (C, C), dtype=jnp.float32) / np.sqrt(C), 'Wv': jax.random.normal(ks[2], (C, C), dtype=jnp.float32) / np.sqrt(C), 'Wr': jax.random.normal(ks[3], (C, C), dtype=jnp.float32) / np.sqrt(C), 'Wo': jax.random.normal(ks[4], (C, C), dtype=jnp.float32) / np.sqrt(C)}
    _L0_attn_in = _L0_attn_setup()

    def _L0_ffn_setup():
        import jax, jax.numpy as jnp
        import numpy as np
        JITTER_EPS = 0.01

        def phi_routing(logits, jitter_eps=JITTER_EPS):
            m, sel = jax.lax.top_k(logits, 2)
            T, E = logits.shape
            m1 = m[:, :1]
            factor1 = jnp.maximum(jnp.abs(logits), m1)
            mask1 = (m1 - logits) / factor1 > 2.0 * jitter_eps
            p1 = jax.nn.softmax(jnp.where(mask1, -jnp.inf, logits), axis=-1)
            mult1 = jnp.take_along_axis(p1, sel[:, :1], axis=-1)
            m2 = m[:, 1:2]
            factor2 = jnp.maximum(jnp.abs(logits), m2)
            mask2 = (m2 - logits) / factor2 > 2.0 * jitter_eps
            drop_top1 = jnp.arange(E)[None, :] == sel[:, :1]
            p2 = jax.nn.softmax(jnp.where(mask2 | drop_top1, -jnp.inf, logits), axis=-1)
            mult2 = jnp.take_along_axis(p2, sel[:, 1:2], axis=-1)
            return (jnp.concatenate([mult1, mult2], axis=-1), sel)
        key = jax.random.key(seed)
        k = jax.random.split(key, 5)
        B, S, H, F, E = (1, 64, 128, 512, 8)
        return {'hidden_states': jax.random.normal(k[0], (B, S, H), jnp.float32), 'gate_w': jax.random.normal(k[1], (E, H), jnp.float32) * 0.02, 'w1': jax.random.normal(k[2], (E, F, H), jnp.float32) * 0.02, 'w2': jax.random.normal(k[3], (E, H, F), jnp.float32) * 0.02, 'w3': jax.random.normal(k[4], (E, F, H), jnp.float32) * 0.02}
    _L0_ffn_in = _L0_ffn_setup()
    _L0_c = _w((lambda *s: np.random.randn(*s).astype(np.float32) * 0.05)(16, 128))
    _L0_wmod = _w((lambda *s: np.random.randn(*s).astype(np.float32) * 0.05)(128, 6 * 128) * 128 ** (-0.5))
    _d = {'L0_attn_x': _L0_attn_in['x'], 'L0_attn_time_decay': _L0_attn_in['time_decay'], 'L0_attn_time_first': _L0_attn_in['time_first'], 'L0_attn_time_mix_k': _L0_attn_in['time_mix_k'], 'L0_attn_time_mix_v': _L0_attn_in['time_mix_v'], 'L0_attn_time_mix_r': _L0_attn_in['time_mix_r'], 'L0_attn_Wk': _L0_attn_in['Wk'], 'L0_attn_Wv': _L0_attn_in['Wv'], 'L0_attn_Wr': _L0_attn_in['Wr'], 'L0_attn_Wo': _L0_attn_in['Wo'], 'L0_ffn_gate_w': _L0_ffn_in['gate_w'], 'L0_ffn_w1': _L0_ffn_in['w1'], 'L0_ffn_w2': _L0_ffn_in['w2'], 'L0_ffn_w3': _L0_ffn_in['w3'], 'L0_c': _L0_c, 'L0_wmod': _L0_wmod}
    _x0 = _d['L0_attn_x']
    _d['L0_attn_x'] = jax.random.normal(jax.random.fold_in(jax.random.key(seed), 1), (16, 256, 128), dtype=_x0.dtype)
    del _x0
    return _d

def reference(L0_attn_x, L0_attn_time_decay, L0_attn_time_first, L0_attn_time_mix_k, L0_attn_time_mix_v, L0_attn_time_mix_r, L0_attn_Wk, L0_attn_Wv, L0_attn_Wr, L0_attn_Wo, L0_ffn_gate_w, L0_ffn_w1, L0_ffn_w2, L0_ffn_w3, L0_c, L0_wmod):

    def _L0_attn_ref(x, time_decay, time_first, time_mix_k, time_mix_v, time_mix_r, Wk, Wv, Wr, Wo):
        import jax, jax.numpy as jnp
        import numpy as np
        B, T, C = (8, 512, 128)

        def _wkv(w_decay, u_first, k, v):
            w = -jnp.exp(w_decay)
            u = u_first
            kt = jnp.transpose(k, (1, 0, 2))
            vt = jnp.transpose(v, (1, 0, 2))
            a0 = jnp.zeros((k.shape[0], k.shape[2]), dtype=k.dtype)
            b0 = jnp.zeros_like(a0)
            p0 = jnp.full_like(a0, -1e+38)

            def step(carry, kv):
                a, b, p = carry
                k_t, v_t = kv
                q = jnp.maximum(p, u + k_t)
                e1 = jnp.exp(p - q)
                e2 = jnp.exp(u + k_t - q)
                y = (e1 * a + e2 * v_t) / (e1 * b + e2)
                q2 = jnp.maximum(p + w, k_t)
                f1 = jnp.exp(p + w - q2)
                f2 = jnp.exp(k_t - q2)
                return ((f1 * a + f2 * v_t, f1 * b + f2, q2), y)
            _, y = jax.lax.scan(step, (a0, b0, p0), (kt, vt))
            return jnp.transpose(y, (1, 0, 2))
        x_prev = jnp.pad(x, ((0, 0), (1, 0), (0, 0)))[:, :-1]
        xk = x_prev + time_mix_k * (x - x_prev)
        xv = x_prev + time_mix_v * (x - x_prev)
        xr = x_prev + time_mix_r * (x - x_prev)
        k = jnp.einsum('btc,dc->btd', xk, Wk)
        v = jnp.einsum('btc,dc->btd', xv, Wv)
        sr = jax.nn.sigmoid(jnp.einsum('btc,dc->btd', xr, Wr))
        wkv = _wkv(time_decay.reshape(-1), time_first.reshape(-1), k, v)
        return jnp.einsum('btc,dc->btd', sr * wkv, Wo)

    def _L0_ffn_ref(hidden_states, gate_w, w1, w2, w3):
        import jax, jax.numpy as jnp
        import numpy as np
        JITTER_EPS = 0.01

        def phi_routing(logits, jitter_eps=JITTER_EPS):
            m, sel = jax.lax.top_k(logits, 2)
            T, E = logits.shape
            m1 = m[:, :1]
            factor1 = jnp.maximum(jnp.abs(logits), m1)
            mask1 = (m1 - logits) / factor1 > 2.0 * jitter_eps
            p1 = jax.nn.softmax(jnp.where(mask1, -jnp.inf, logits), axis=-1)
            mult1 = jnp.take_along_axis(p1, sel[:, :1], axis=-1)
            m2 = m[:, 1:2]
            factor2 = jnp.maximum(jnp.abs(logits), m2)
            mask2 = (m2 - logits) / factor2 > 2.0 * jitter_eps
            drop_top1 = jnp.arange(E)[None, :] == sel[:, :1]
            p2 = jax.nn.softmax(jnp.where(mask2 | drop_top1, -jnp.inf, logits), axis=-1)
            mult2 = jnp.take_along_axis(p2, sel[:, 1:2], axis=-1)
            return (jnp.concatenate([mult1, mult2], axis=-1), sel)
        B, S, H = hidden_states.shape
        E = w1.shape[0]
        x = hidden_states.reshape(-1, H)
        logits = x @ gate_w.T
        routing_weights, selected = phi_routing(logits)
        T = x.shape[0]
        wte = jnp.zeros((T, E), x.dtype).at[jnp.arange(T)[:, None], selected].add(routing_weights)
        out = jnp.zeros_like(x)
        for e in range(E):
            h = jax.nn.silu(x @ w1[e].T) * (x @ w3[e].T)
            out = out + wte[:, e:e + 1] * (h @ w2[e].T)
        return out.reshape(B, S, H)
    x = L0_attn_x
    mod = (_silu(L0_c) @ L0_wmod).reshape(L0_c.shape[0], 6, 1, -1)
    sa, ca, ga, sb, cb, gb = (mod[:, 0], mod[:, 1], mod[:, 2], mod[:, 3], mod[:, 4], mod[:, 5])
    ga = (2 * (ga >= 0) - 1) * jnp.maximum(jnp.abs(ga), 0.25)
    gb = (2 * (gb >= 0) - 1) * jnp.maximum(jnp.abs(gb), 0.25)
    h = _layernorm(x, axis=-1) * (1 + ca) + sa
    x = x + ga * _L0_attn_ref(h, L0_attn_time_decay, L0_attn_time_first, L0_attn_time_mix_k, L0_attn_time_mix_v, L0_attn_time_mix_r, L0_attn_Wk, L0_attn_Wv, L0_attn_Wr, L0_attn_Wo)
    h = _layernorm(x, axis=-1) * (1 + cb) + sb
    x = x + gb * _L0_ffn_ref(h, L0_ffn_gate_w, L0_ffn_w1, L0_ffn_w2, L0_ffn_w3)
    return x

_drawn_inputs = setup_inputs


def setup_inputs(seed=0):
    import zlib

    import numpy as np

    out = dict(_drawn_inputs(seed))
    spreads = {}
    factors = {'L0_attn_time_decay': 6.445,
     'L0_attn_time_first': 6.385,
     'L0_attn_time_mix_k': 2.713,
     'L0_attn_time_mix_r': 3.431,
     'L0_ffn_gate_w': 8.0,
     'L0_ffn_w1': 8.0,
     'L0_ffn_w2': 8.0,
     'L0_ffn_w3': 8.0}
    for name, (base, spread) in spreads.items():
        noise = np.random.default_rng([zlib.crc32(name.encode()), seed]).standard_normal(out[name].shape)
        drawn = base * np.exp(spread * noise) if base else spread * noise
        out[name] = jnp.asarray(drawn.astype(out[name].dtype))
    for name, factor in factors.items():
        out[name] = (out[name] * factor).astype(out[name].dtype)
    return out
```

```python
from contextlib import ExitStack

import concourse.bass as bass
from concourse import mybir

F32 = mybir.dt.float32
BF16 = mybir.dt.bfloat16
I32 = mybir.dt.int32
U32 = mybir.dt.uint32
ALU = mybir.AluOpType
ACT = mybir.ActivationFunctionType
AX_X = mybir.AxisListType.X

P = 128
B, T, C = 16, 256, 128
TOKENS = B * T
E, F = 8, 512
FB = F // P
CHUNK = 512
SEQS = CHUNK // T
TILES = CHUNK // P
NCH = TOKENS // CHUNK
PAIRT = 2 * TILES
REGION = TOKENS + P
DUMMY = E * REGION
ROW = C + 2
NT = 72
RING = 8
PAIR_DMAS = 16 * 2 * TILES
NEG = -1e38
DROP = -3e38
NOWHERE = 1 << 20
EPS = 1e-5
JITTER2 = 0.02
assert (2 * TOKENS + E * (P - 1)) // P <= NT and NT % RING == 0


def bc(ap, axis, n):
    u = ap.unsqueeze(axis)
    shape = list(u.shape)
    shape[axis] = n
    return u.to_broadcast(shape)


def block_program(nc, x_d, par_d, wproj_d, gatew_d, w1_d, w3_d, w2_d, cT_d, wmod_d, out_d):
    with ExitStack() as ctx:
        def sb(name, shape, dt=F32):
            return ctx.enter_context(nc.sbuf_tensor(name, shape, dt))

        sems = {}

        def S(name):
            if name not in sems:
                sems[name] = ctx.enter_context(nc.semaphore(name))
            return sems[name]

        rows_d = nc.dram_tensor("expert_rows", [DUMMY + P, ROW], F32, kind="Internal").ap()
        y_d = nc.dram_tensor("choice_rows", [2 * TOKENS, C], F32, kind="Internal").ap()
        gates_d = nc.dram_tensor("gate_scratch", [B, 2 * C], F32, kind="Internal").ap()

        bank = [ctx.enter_context(nc.psum_tensor(f"bank{i}", [P, 512], F32)) for i in range(8)]
        pK, pV, pR, pXn, pXn2, pBack, pAttn, pSmall = bank
        pGate, pUp, pHt, pXt, pY = bank[0:2], bank[2:4], bank[4:6], bank[6], bank[7]
        pLogit = pSmall[:, 0:TILES * E]
        pRank = pSmall[:, 64:64 + PAIRT * E]
        pCount = pSmall[:, 192:192 + E]

        ident = sb("ident", [P, P])
        before = sb("before", [P, P], BF16)
        ones = sb("ones", [P, P], BF16)
        ones8 = sb("ones8", [P, E])
        eps = sb("eps", [P, 1])
        par = sb("par", [P, 5])
        wproj = sb("wproj", [P, 4, C])
        wnow = sb("wnow", [P, 3, C])
        wprev = sb("wprev", [P, 3, C])
        gatew = sb("gatew", [P, E])
        w1 = sb("w1", [P, E * F])
        w3 = sb("w3", [P, E * F])
        w2 = sb("w2", [P, E * F])
        cT = sb("cT", [P, B])
        cexp = sb("cexp", [P, B])
        cinv = sb("cinv", [P, B])
        csilu = sb("csilu", [P, B])
        wmod = sb("wmod", [P, 6 * C])
        mods = sb("mods", [P, 4, B])
        gsign = sb("gsign", [B, 2 * C])
        gabs = sb("gabs", [B, 2 * C])
        graw = sb("graw", [B, 2 * C])
        gone = sb("gone", [B, 2 * C])
        gfix = sb("gfix", [B, 2 * C])
        gates = sb("gates", [P, B, 2, C])
        wog = sb("wog", [P, B, C])
        edecay = sb("edecay", [P, 1])
        wdecay = sb("wdecay", [P, 1])
        prio = sb("prio", [P, E])
        ereg = sb("ereg", [P, E])
        eoff = sb("eoff", [P, E])
        thr = sb("thr", [P, TOKENS // P])
        pcol = sb("pcol", [P, 2])
        ids = sb("ids", [P, 2, TOKENS // P], I32)
        padrow = sb("padrow", [P, ROW])

        xs = sb("xs", [P, TOKENS // P, C])
        bn1 = sb("bn1", [P, TILES, 6])
        mv1 = sb("mv1", [P, TILES, 2])
        lnv1 = sb("lnv1", [P, TILES])
        rstd1 = sb("rstd1", [P, TILES])
        bn2 = sb("bn2", [P, TILES, 6])
        mv2 = sb("mv2", [P, TILES, 2])
        lnv2 = sb("lnv2", [P, TILES])
        rstd2 = sb("rstd2", [P, TILES])
        xn = sb("xn", [P, TILES, C])
        xn2 = sb("xn2", [P, TILES, C])
        hT = sb("hT", [P, SEQS, T + 1])
        h2T = sb("h2T", [P, CHUNK])
        pmax = sb("pmax", [P, SEQS, T + 1])
        z = sb("z", [P, CHUNK])
        arg = sb("arg", [P, 4, CHUNK])
        fac = sb("fac", [P, 4, CHUNK])
        fv = sb("fv", [P, CHUNK])
        ev = sb("ev", [P, CHUNK])
        sa_ = sb("state_a", [P, CHUNK + 1])
        sb_ = sb("state_b", [P, CHUNK + 1])
        num0 = sb("num0", [P, CHUNK])
        num = sb("num", [P, CHUNK])
        den0 = sb("den0", [P, CHUNK])
        den1 = sb("den1", [P, CHUNK])
        den = sb("den", [P, CHUNK])
        rabs = sb("rabs", [P, CHUNK])
        rexp = sb("rexp", [P, CHUNK])
        lden = sb("lden", [P, CHUNK])
        garg = sb("garg", [P, CHUNK])
        gfac = sb("gfac", [P, CHUNK])
        yT = sb("yT", [P, CHUNK])
        hrow = sb("hrow", [P, 2, 2, TILES, ROW])

        LL = sb("LL", [P, 2, PAIRT, E])
        top = sb("top", [P, 2, PAIRT])
        eq = sb("eq", [P, 2, PAIRT, E])
        pick = sb("pick", [P, 2, PAIRT, E])
        pbest = sb("pbest", [P, 2, PAIRT])
        hot = sb("hot", [P, 2, PAIRT, E])
        hots = sb("hots", [P, PAIRT, E], BF16)
        dif = sb("dif", [P, 2, PAIRT, E])
        mag = sb("mag", [P, 2, PAIRT, E])
        lim = sb("lim", [P, 2, PAIRT, E])
        keep = sb("keep", [P, 2, PAIRT, E])
        dexp = sb("dexp", [P, 2, PAIRT, E])
        kexp = sb("kexp", [P, 2, PAIRT, E])
        ksum = sb("ksum", [P, 2, PAIRT])
        base = sb("base", [P, E])
        pos = sb("pos", [P, PAIRT, E])
        hpos = sb("hpos", [P, 2, PAIRT, E])
        slot = sb("slot", [P, 2, PAIRT], I32)

        cnt = sb("cnt", [P, E])
        more = sb("more", [P, E, TOKENS // P])
        ntile = sb("ntile", [P, E])
        tend = sb("tend", [P, E])
        tstart = sb("tstart", [P, E])
        padidx = sb("padidx", [P, E], I32)
        started = sb("started", [P, E])
        ended = sb("ended", [P, E])
        inside = sb("inside", [P, E])
        rbase = sb("rbase", [P, E])
        rowv = sb("rowv", [P, E])
        prod = sb("prod", [P, 2, E])
        sums = sb("sums", [P, 2])
        plan = sb("plan", [P, 2])
        table = sb("table", [1, 2, NT], I32)

        X = [sb(f"X{i}", [P, ROW]) for i in range(RING)]
        xT = [sb(f"xT{i}", [P, P]) for i in range(2)]
        sg = [sb(f"sg{i}", [P, F]) for i in range(2)]
        hh = [sb(f"hh{i}", [P, F]) for i in range(2)]
        hhT = [sb(f"hhT{i}", [P, F]) for i in range(2)]
        yy = [sb(f"yy{i}", [P, C]) for i in range(RING)]
        ych = [w[:].rearrange("p (k c) -> p k c", c=C) for w in (w1, w3)]
        fsum = sb("fsum", [P, 2, TILES, C])
        fgat = sb("fgat", [P, 2, TILES, C])

        f1, e1, f2, e2 = (fac[:, i, :] for i in range(4))
        seq2 = lambda ap: ap.rearrange("p (s t) -> p s t", s=SEQS)
        til = lambda ap: ap.rearrange("p (k c) -> p k c", k=TILES)

        def settle(eng):
            eng.sem_inc(S(f"settled_{eng.engine.name}"), 1)

        block = ctx.enter_context(nc.Block())

        def front(eng, step):
            step(0, 0)
            with eng.Fori(0, (NCH - 2) // 2, 1) as i:
                step(i * 2 + 1, 1)
                step(i * 2 + 2, 0)
            step(NCH - 1, 1)
            step(NCH, 0)

        @block.sync
        def _(sp):
            xv = x_d.rearrange("b (h p) c -> p (b h) c", p=P)
            cut = 2 * TILES
            sp.dma_start(xs[:, 0:cut, :], xv[:, 0:cut, :]).then_inc(S("x_head"), 16)
            sp.dma_start(cT[:], cT_d).then_inc(S("cond_loaded"), 16)
            sp.dma_start(wmod[:], wmod_d).then_inc(S("cond_loaded"), 16)
            sp.dma_start(par[:], par_d).then_inc(S("par_loaded"), 16)
            sp.dma_start(wproj[:], wproj_d).then_inc(S("par_loaded"), 16)
            sp.dma_start(xs[:, cut:, :], xv[:, cut:, :]).then_inc(S("x_rest"), 16)
            sp.dma_start(gatew[:], gatew_d).then_inc(S("gatew_loaded"), 16)
            sp.wait_ge(S("gfix_ready"), 1)
            sp.dma_start(gates_d, gfix[:]).then_inc(S("gates_stored"), 16)
            sp.wait_ge(S("gates_stored"), 16)
            sp.dma_start(gates[:].rearrange("p b g c -> p (b g c)"),
                         gates_d.rearrange("b g -> (b g)").partition_broadcast(P)).then_inc(S("gates_loaded"), 16)
            sp.wait_ge(S("padrow_ready"), 2)
            sp.dma_start(rows_d[DUMMY:DUMMY + P, :], padrow[:]).then_inc(S("dummy_stored"), 16)
            sp.dma_start(w1[:], w1_d).then_inc(S("experts_loaded"), 16)
            sp.dma_start(w3[:], w3_d).then_inc(S("experts_loaded"), 16)
            sp.dma_start(w2[:], w2_d).then_inc(S("experts_loaded"), 16)

            sp.wait_ge(S("dummy_stored"), 16)
            sp.wait_ge(S("pads_landed"), 16 * E)
            sp.wait_ge(S("rows_landed0"), PAIR_DMAS * NCH // 2)
            sp.wait_ge(S("rows_landed1"), PAIR_DMAS * NCH // 2)
            sp.wait_ge(S("table_ready"), 1)

            def load_tile(j, b):
                row = sp.value_load(table[0:1, 0, bass.ds(j, 1)], min_val=0, max_val=DUMMY)
                sp.dma_start(X[b][:], rows_d[bass.ds(row, P), :]).then_inc(S(f"tile_loaded{b}"), 16)

            for b in range(RING):
                load_tile(b, b)
            with sp.Fori(1, NT // RING, 1) as i:
                for b in range(RING):
                    sp.wait_ge(S(f"y_landed{b}"), i * 16)
                    load_tile(i * RING + b, b)

            for b in range(RING):
                sp.wait_ge(S(f"y_landed{b}"), 16 * NT // RING)
            yv = y_d.rearrange("(g k p) c -> p g k c", g=2, p=P)
            for c in range(NCH):
                for g in range(2):
                    sp.dma_start(ych[g][:, c * TILES:(c + 1) * TILES, :],
                                 yv[:, g, c * TILES:(c + 1) * TILES, :]).then_inc(S(f"y_loaded{c}"), 16)
            ov = out_d.rearrange("b (h p) c -> p (b h) c", p=P)
            for c in range(NCH):
                sp.wait_ge(S("out_ready"), c + 1)
                sp.dma_start(ov[:, c * TILES:(c + 1) * TILES, :],
                             xs[:, c * TILES:(c + 1) * TILES, :]).then_inc(S("out_stored"), 16)
            sp.wait_ge(S("out_stored"), 16 * NCH)

        @block.gpsimd
        def _(pool):
            pool.memset(ident[:], 0.0).then_inc(S("blank"), 1)
            pool.memset(before[:], 1.0).then_inc(S("blank"), 1)
            pool.memset(ones[:], 1.0).then_inc(S("ones_ready"), 1)
            pool.wait_ge(S("blank"), 2)
            pool.affine_select(out=ident[:], in_=ident[:], compare_op=ALU.not_equal, fill=1.0, base=0,
                               pattern=[[-1, P]], channel_multiplier=1).then_inc(S("ident_ready"), 1)
            pool.affine_select(out=before[:], in_=before[:], compare_op=ALU.is_gt, fill=0.0, base=0,
                               pattern=[[1, P]], channel_multiplier=-1).then_inc(S("before_ready"), 1)
            fl = dict(allow_small_or_imprecise_dtypes=True)
            pool.iota(prio[:], [[-1, E]], base=E, channel_multiplier=0, **fl).then_inc(S("tables"), 1)
            pool.iota(ereg[:], [[REGION, E]], base=0, channel_multiplier=0, **fl).then_inc(S("tables"), 1)
            pool.iota(eoff[:], [[F, E]], base=0, channel_multiplier=0, **fl).then_inc(S("tables"), 1)
            pool.iota(base[:], [[REGION, E]], base=0, channel_multiplier=0, **fl).then_inc(S("tables"), 1)
            pool.iota(thr[:], [[P, TOKENS // P]], base=0, channel_multiplier=0, **fl).then_inc(S("tables"), 1)
            pool.iota(pcol[:, 0:1], [[0, 1]], base=0, channel_multiplier=1, **fl).then_inc(S("tables"), 1)
            pool.iota(pcol[:, 1:2], [[0, 1]], base=0, channel_multiplier=P, **fl).then_inc(S("tables"), 1)
            pool.iota(ids[:], [[TOKENS, 2], [P, TOKENS // P]], base=0, channel_multiplier=1).then_inc(S("ids_ready"), 1)
            pool.memset(padrow[:], 0.0).then_inc(S("padrow_ready"), 1)
            pool.wait_ge(S("padrow_ready"), 1)
            pool.iota(padrow[:, C:C + 1].bitcast(I32), [[0, 1]], base=NOWHERE, channel_multiplier=0)\
                .then_inc(S("padrow_ready"), 1)
            pool.wait_ge(S("gates_loaded"), 16)
            pool.wait_ge(S("par_loaded"), 32)
            pool.tensor_tensor(wog[:], bc(wproj[:, 3, :], 1, B), gates[:, :, 0, :], ALU.mult)\
                .then_inc(S("wog_ready"), 1)
            pool.wait_ge(S("ids_ready"), 1)

            def address(q):
                for h in range(2):
                    pool.tensor_copy(hrow[:, h, :, :, C].bitcast(I32),
                                     ids[:, :, bass.ds(q * PAIRT + h * TILES, TILES)]).then_inc(S(f"dest_ready{h}"), 1)

            def scatter(q):
                for h in range(2):
                    pool.wait_ge(S(f"dest_ready{h}"), q + 1)
                pool.wait_ge(S("slots_ready"), q + 1)
                pool.wait_ge(S("rows_ready"), q * 2 + 2)
                settle(pool)
                for h in range(2):
                    for k in range(TILES):
                        for g in range(2):
                            t = h * TILES + k
                            pool.indirect_dma_start(
                                rows_d, bass.IndirectOffsetOnAxis(ap=slot[:, g, t:t + 1].bitcast(U32), axis=0),
                                hrow[:, h, g, k, :], None).then_inc(S(f"rows_landed{h}"), 16)

            address(0)
            with pool.Fori(0, NCH // 2 - 1, 1) as q:
                scatter(q)
                for h in range(2):
                    pool.wait_ge(S(f"rows_landed{h}"), q * PAIR_DMAS + PAIR_DMAS)
                settle(pool)
                address(q + 1)
            scatter(NCH // 2 - 1)
            pool.wait_ge(S("pads_ready"), 1)
            for e in range(E):
                pool.indirect_dma_start(
                    rows_d, bass.IndirectOffsetOnAxis(ap=padidx[:, e:e + 1].bitcast(U32), axis=0),
                    padrow[:], None).then_inc(S("pads_landed"), 16)
            with pool.Fori(0, NT // RING, 1) as i:
                for b in range(RING):
                    pool.wait_ge(S("y_ready"), i * RING + (b + 1))
                    settle(pool)
                    pool.indirect_dma_start(
                        y_d, bass.IndirectOffsetOnAxis(ap=X[b][:, C:C + 1].bitcast(U32), axis=0), yy[b][:], None,
                        bounds_check=2 * TOKENS - 1, oob_is_err=False).then_inc(S(f"y_landed{b}"), 16)

        @block.tensor
        def _(pe):
            pe.wait_ge(S("cond_loaded"), 32)
            pe.wait_ge(S("csilu_ready"), 1)
            for n, j in enumerate((0, 1, 3, 4)):
                pe.matmul(pAttn[:, n * B:(n + 1) * B], wmod[:, j * C:(j + 1) * C], csilu[:], start=True, stop=True)
            for n, j in enumerate((2, 5)):
                m = pe.matmul(pBack[0:B, n * C:(n + 1) * C], csilu[:], wmod[:, j * C:(j + 1) * C],
                              start=True, stop=True)
            m.then_inc(S("mods_ready"), 1)
            pe.wait_ge(S("ident_ready"), 1)

            def turn1(c, first=False):
                pe.wait_ge(S("xn_ready"), c + 1)
                if not first:
                    pe.wait_ge(S("hT_ready"), c)
                for k in range(TILES):
                    m = pe.transpose(pXn[:, k * P:(k + 1) * P], xn[:, k, :], ident[:])
                m.then_inc(S("xnT_ready"), 1)

            def project(c, n, dst, done):
                pe.matmul(seq2(dst[:]), wnow[:, n, :], hT[:, :, 1:], start=True, stop=False)
                pe.matmul(seq2(dst[:]), wprev[:, n, :], hT[:, :, 0:T], start=False, stop=True).then_inc(S(done), 1)

            def proj_k(c, first=False):
                pe.wait_ge(S("hT_ready"), c + 1)
                if not first:
                    pe.wait_ge(S("z_ready"), c)
                project(c, 0, pK, "k_ready")

            def proj_v(c, first=False):
                if not first:
                    pe.wait_ge(S("vprods_ready"), c)
                project(c, 1, pV, "v_ready")

            def proj_r(c, first=False):
                if not first:
                    pe.wait_ge(S("garg_ready"), c)
                project(c, 2, pR, "r_ready")

            def step(c, parity):
                is0 = isinstance(c, int) and c == 0
                last = isinstance(c, int) and c >= NCH - 1
                ends = isinstance(c, int) and c == NCH
                if not last:
                    turn1(c + 1)
                if not is0:
                    pe.wait_ge(S("xn2_ready"), c)
                    for k in range(TILES):
                        m = pe.transpose(pXn2[:, k * P:(k + 1) * P], xn2[:, k, :], ident[:])
                    m.then_inc(S("xn2T_ready"), 1)
                if not last:
                    proj_k(c + 1)
                if not is0:
                    pe.wait_ge(S("h2T_ready"), c)
                    for k in range(TILES):
                        m = pe.matmul(pLogit[:, k * E:(k + 1) * E], h2T[:, k * P:(k + 1) * P], gatew[:],
                                      start=True, stop=True)
                    m.then_inc(S("logits_ready"), 1)
                    for k in range(TILES):
                        m = pe.transpose(pBack[:, k * P:(k + 1) * P], h2T[:, k * P:(k + 1) * P], ident[:])
                    m.then_inc(S("back_ready"), 1)
                if not last:
                    proj_v(c + 1)
                    proj_r(c + 1)
                if not ends:
                    pe.wait_ge(S("yT_ready"), c + 1)
                    for k in range(TILES):
                        m = pe.matmul(pAttn[:, k * P:(k + 1) * P], yT[:, k * P:(k + 1) * P],
                                      wog[:, bass.ds(c * SEQS + k // (TILES // SEQS), 1), :],
                                      start=True, stop=True)
                    m.then_inc(S("attn_ready"), 1)
                if parity == 0 and not is0:
                    q1 = c // 2 if isinstance(c, int) else step.pairs + 1
                    pe.wait_ge(S("hots_ready"), q1)
                    hv = hots[:].rearrange("p t e -> p (t e)")
                    pe.matmul(pRank, before[:], hv, start=True, stop=False)
                    for d in range(1, PAIRT):
                        m = pe.matmul(pRank[:, d * E:], ones[:], hv[:, 0:(PAIRT - d) * E],
                                      start=False, stop=d == PAIRT - 1)
                    for t in range(PAIRT):
                        m = pe.matmul(pCount, ones[:], hots[:, t, :], start=t == 0, stop=t == PAIRT - 1)
                    m.then_inc(S("ranks_ready"), 1)

            pe.wait_ge(S("proj_ready"), 1)
            turn1(0, first=True)
            proj_k(0, first=True)
            proj_v(0, first=True)
            proj_r(0, first=True)
            pe.wait_ge(S("gatew_loaded"), 16)
            pe.wait_ge(S("wog_ready"), 1)
            pe.wait_ge(S("before_ready"), 1)
            pe.wait_ge(S("ones_ready"), 1)
            step(0, 0)
            with pe.Fori(0, (NCH - 2) // 2, 1) as i:
                step.pairs = i
                step(i * 2 + 1, 1)
                step(i * 2 + 2, 0)
            step(NCH - 1, 1)
            step(NCH, 0)

            pe.wait_ge(S("plan_ready"), 1)
            for n in range(2):
                m = pe.transpose(pSmall[0:1, 256 + n * NT:256 + (n + 1) * NT], plan[0:NT, n:n + 1], ident[0:NT, 0:NT])
            m.then_inc(S("planT_ready"), 1)

            pe.wait_ge(S("table_ready"), 1)
            pe.wait_ge(S("experts_loaded"), 48)

            def turn_x(j, b, u, first=False):
                pe.wait_ge(S(f"tile_loaded{b}"), u)
                if not first:
                    pe.wait_ge(S("xT_ready"), j)
                pe.transpose(pXt[:, 0:P], X[b][:, 0:C], ident[:]).then_inc(S("tile_turned"), 1)

            def gate_up(j, b, first=False):
                off = pe.value_load(table[0:1, 1, bass.ds(j, 1)], min_val=0, max_val=(E - 1) * F)
                pe.wait_ge(S("xT_ready"), j + 1)
                if not first:
                    pe.wait_ge(S("h_ready"), j - 1)
                pe.matmul(pGate[b % 2][:], xT[b % 2][:], w1[:, bass.ds(off, F)], start=True, stop=True)\
                    .then_inc(S("gate_ready"), 1)
                pe.matmul(pUp[b % 2][:], xT[b % 2][:], w3[:, bass.ds(off, F)], start=True, stop=True)\
                    .then_inc(S("up_ready"), 1)

            def turn_h(j, b, first=False):
                pe.wait_ge(S("h_ready"), j + 1)
                if not first:
                    pe.wait_ge(S("hT_done"), j - 1)
                for k in range(FB):
                    m = pe.transpose(pHt[b % 2][:, k * P:(k + 1) * P], hh[b % 2][:, k * P:(k + 1) * P], ident[:])
                m.then_inc(S("h_turned"), 1)

            def down(j, b, first=False):
                off = pe.value_load(table[0:1, 1, bass.ds(j, 1)], min_val=0, max_val=(E - 1) * F)
                pe.wait_ge(S("hT_done"), j + 1)
                if not first:
                    pe.wait_ge(S("y_ready"), j)
                for k in range(FB):
                    m = pe.matmul(pY[:, 0:C], hhT[b % 2][:, k * P:(k + 1) * P], w2[:, bass.ds(off + k * P, P)],
                                  start=k == 0, stop=k == FB - 1)
                m.then_inc(S("down_ready"), 1)

            def loads(j):
                return 16 * (j // RING + 1)

            def tile_step(s, b):
                flat = isinstance(s, int)
                if not flat or s < NT:
                    gate_up(s, b, first=flat and s < 2)
                if not flat or s + 1 < NT:
                    turn_x(s + 1, (b + 1) % RING, loads(s + 1) if flat else i * 16 + 32 + 16 * ((b + 1) // RING))
                if not flat or 0 <= s - 1 < NT:
                    turn_h(s - 1, (b - 1) % RING, first=flat and s < 3)
                if not flat or s >= 2:
                    down(s - 2, (b - 2) % RING, first=flat and s < 3)

            turn_x(0, 0, loads(0), first=True)
            for s in range(RING):
                tile_step(s, s)
            with pe.Fori(0, NT // RING - 2, 1) as i:
                for b in range(RING):
                    tile_step(i * RING + (RING + b), b)
            for s in range(NT - RING, NT + 2):
                tile_step(s, s % RING)

        @block.scalar
        def _(act):
            act.preload_act_table_set("natural_log_exp_and_others")
            act.wait_ge(S("cond_loaded"), 32)
            act.activation(cexp[:], cT[:], ACT.Exp, scale=-1.0).then_inc(S("cexp_ready"), 1)
            act.wait_ge(S("par_loaded"), 32)
            act.activation(edecay[:], par[:, 0:1], ACT.Exp).then_inc(S("edecay_ready"), 1)
            act.wait_ge(S("eps_ready"), 1)

            def inv_std(c, mv, lnv, rstd, moments, logged, ready):
                act.wait_ge(S(moments), c + 1)
                act.activation(lnv[:], mv[:, :, 1], ACT.Ln, bias=eps[:, 0:1]).then_inc(S(logged), 1)
                act.wait_ge(S(logged), c + 1)
                act.activation(rstd[:], lnv[:], ACT.Exp, scale=-0.5).then_inc(S(ready), 1)

            def std1(c):
                inv_std(c, mv1, lnv1, rstd1, "moments1_ready", "lnv1_ready", "rstd1_ready")

            def std2(c):
                inv_std(c, mv2, lnv2, rstd2, "moments2_ready", "lnv2_ready", "rstd2_ready")

            def modulate1(c, first=False):
                act.wait_ge(S("xnT_ready"), c + 1)
                if not first:
                    act.wait_ge(S("r_ready"), c)
                for s in range(SEQS):
                    m = act.activation(hT[:, s, 1:], pXn[:, s * T:(s + 1) * T], ACT.Identity,
                                       scale=mods[:, 1, bass.ds(c * SEQS + s, 1)],
                                       bias=mods[:, 0, bass.ds(c * SEQS + s, 1)])
                m.then_inc(S("hT_ready"), 1)

            def modulate2(c):
                act.wait_ge(S("xn2T_ready"), c + 1)
                for s in range(SEQS):
                    m = act.activation(h2T[:, s * T:(s + 1) * T], pXn2[:, s * T:(s + 1) * T], ACT.Identity,
                                       scale=mods[:, 3, bass.ds(c * SEQS + s, 1)],
                                       bias=mods[:, 2, bass.ds(c * SEQS + s, 1)])
                m.then_inc(S("h2T_ready"), 1)

            def step(c, parity):
                is0 = isinstance(c, int) and c == 0
                last = isinstance(c, int) and c >= NCH - 1
                ends = isinstance(c, int) and c == NCH
                if not last:
                    std1(c + 1)
                if not is0:
                    std2(c - 1)
                if not ends:
                    act.wait_ge(S("args_ready"), c * 2 + 1)
                    act.activation(fac[:, 0:2, :], arg[:, 0:2, :], ACT.Exp, scale=-1.0).then_inc(S("facs_ready"), 1)
                    act.wait_ge(S("args_ready"), c * 2 + 2)
                    act.activation(fac[:, 2:4, :], arg[:, 2:4, :], ACT.Exp).then_inc(S("facs_ready"), 1)
                    act.wait_ge(S("r_ready"), c + 1)
                    act.activation(rabs[:], pR[:], ACT.Abs).then_inc(S("rabs_ready"), 1)
                    act.wait_ge(S("rabs_ready"), c + 1)
                    act.activation(rexp[:], rabs[:], ACT.Exp, scale=-1.0).then_inc(S("rexp_ready"), 1)
                if not last:
                    modulate1(c + 1)
                if not is0:
                    modulate2(c - 1)
                if not ends:
                    act.wait_ge(S("den_ready"), c + 1)
                    act.activation(lden[:], den[:], ACT.Ln).then_inc(S("lden_ready"), 1)
                if not is0:
                    act.wait_ge(S("back_ready"), c)
                    half = (parity + 1) % 2
                    sent = (c - 1) // 2 if isinstance(c, int) else step.pairs
                    act.wait_ge(S(f"dest_ready{half}"), sent + 1)
                    for g in range(2):
                        m = act.activation(hrow[:, half, g, :, 0:C], til(pBack[:]), ACT.Copy)
                    m.then_inc(S("rows_ready"), 1)
                if not ends:
                    act.wait_ge(S("garg_ready"), c + 1)
                    act.activation(gfac[:], garg[:], ACT.Exp).then_inc(S("gfac_ready"), 1)
                if parity == 0 and not is0:
                    q1 = c // 2 if isinstance(c, int) else step.pairs + 1
                    act.wait_ge(S("dif_ready"), q1)
                    act.activation(dexp[:], dif[:], ACT.Exp).then_inc(S("dexp_ready"), 1)

            std1(0)
            act.wait_ge(S("mods_fixed"), 1)
            modulate1(0, first=True)
            step(0, 0)
            with act.Fori(0, (NCH - 2) // 2, 1) as i:
                step.pairs = i
                step(i * 2 + 1, 1)
                step(i * 2 + 2, 0)
            step(NCH - 1, 1)
            step(NCH, 0)

            act.preload_act_table(ACT.Silu)

            def take_x(j, b, first=False):
                act.wait_ge(S("tile_turned"), j + 1)
                if not first:
                    act.wait_ge(S("up_ready"), j - 1)
                act.activation(xT[b % 2][:], pXt[:, 0:P], ACT.Copy).then_inc(S("xT_ready"), 1)

            def silu(j, b, first=False):
                act.wait_ge(S("gate_ready"), j + 1)
                if not first:
                    act.wait_ge(S("h_ready"), j - 1)
                act.activation(sg[b % 2][:], pGate[b % 2][:], ACT.Silu).then_inc(S("silu_ready"), 1)

            def weigh(j, b):
                act.wait_ge(S("down_ready"), j + 1)
                act.activation(yy[b][:], pY[:, 0:C], ACT.Copy, scale=X[b][:, C + 1:C + 2]).then_inc(S("y_ready"), 1)

            def tile_step(s, b):
                flat = isinstance(s, int)
                if not flat or s < NT:
                    silu(s, b, first=flat and s < 2)
                if not flat or s + 1 < NT:
                    take_x(s + 1, (b + 1) % RING, first=flat and s < 1)
                if not flat or s >= 2:
                    weigh(s - 2, (b - 2) % RING)

            take_x(0, 0, first=True)
            for s in range(RING):
                tile_step(s, s)
            with act.Fori(0, NT // RING - 2, 1) as i:
                for b in range(RING):
                    tile_step(i * RING + (RING + b), b)
            for s in range(NT - RING, NT + 2):
                tile_step(s, s % RING)

        @block.vector
        def _(dve):
            dve.memset(eps[:], EPS).then_inc(S("eps_ready"), 1)
            dve.memset(hT[:, :, 0], 0.0)
            dve.memset(pmax[:, :, 0], NEG)
            dve.memset(sa_[:, 0:1], 0.0)
            dve.memset(sb_[:, 0:1], 0.0)
            dve.memset(ones8[:], 1.0).then_inc(S("edges_ready"), 1)
            dve.wait_ge(S("cexp_ready"), 1)
            dve.tensor_scalar_add(cinv[:], cexp[:], 1.0).then_inc(S("cond"), 1)
            dve.wait_ge(S("cond"), 1)
            dve.reciprocal(cinv[:], cinv[:]).then_inc(S("cond"), 1)
            dve.wait_ge(S("cond"), 2)
            dve.tensor_tensor(csilu[:], cT[:], cinv[:], ALU.mult).then_inc(S("csilu_ready"), 1)

            def stats(c, bn, mv, told, ready):
                for k in range(TILES):
                    m = dve.bn_stats(bn[:, k, :], xs[:, bass.ds(c * TILES + k, 1), :])
                m.then_inc(S(told), 1)
                dve.wait_ge(S(told), c + 1)
                settle(dve)
                for k in range(TILES):
                    m = dve.bn_aggr(mv[:, k, :], bn[:, k, :])
                m.then_inc(S(ready), 1)

            def stats1(c):
                stats(c, bn1, mv1, "stats1", "moments1_ready")

            def stats2(c):
                stats(c, bn2, mv2, "stats2", "moments2_ready")

            def norm(c, dst, mv, rstd, ready):
                for k in range(TILES):
                    m = dve.tensor_scalar(dst[:, k, :], xs[:, bass.ds(c * TILES + k, 1), :], mv[:, k, 0:1],
                                          rstd[:, k:k + 1], ALU.subtract, ALU.mult)
                m.then_inc(S(ready), 1)

            def norm1(c, first=False):
                dve.wait_ge(S("rstd1_ready"), c + 1)
                if not first:
                    dve.wait_ge(S("xnT_ready"), c)
                norm(c, xn, mv1, rstd1, "xn_ready")

            def norm2(c):
                dve.wait_ge(S("rstd2_ready"), c + 1)
                norm(c, xn2, mv2, rstd2, "xn2_ready")

            dve.wait_ge(S("x_head"), 16)
            stats1(0)
            norm1(0, first=True)
            dve.wait_ge(S("mods_ready"), 1)
            mp = pAttn[:, 0:4 * B].rearrange("p (m b) -> p m b", m=4)
            for m_, one in ((0, 0.0), (1, 1.0), (2, 0.0), (3, 1.0)):
                m = dve.tensor_scalar_add(mods[:, m_, :], mp[:, m_, :], one)
            m.then_inc(S("mods_fixed"), 1)
            gp = pBack[0:B, 0:2 * C]
            dve.tensor_scalar(gsign[:], gp, 0.0, 2.0, ALU.is_ge, ALU.mult).then_inc(S("gate_parts"), 1)
            dve.tensor_copy(graw[:], gp).then_inc(S("gate_parts"), 1)
            dve.wait_ge(S("gate_parts"), 2)
            dve.scalar_tensor_tensor(gabs[:], graw[:], -1.0, graw[:], ALU.mult, ALU.max).then_inc(S("gate_parts"), 1)
            dve.tensor_scalar_add(gone[:], gsign[:], -1.0).then_inc(S("gate_parts"), 1)
            dve.wait_ge(S("gate_parts"), 4)
            dve.scalar_tensor_tensor(gfix[:], gabs[:], 0.25, gone[:], ALU.max, ALU.mult).then_inc(S("gfix_ready"), 1)
            dve.wait_ge(S("par_loaded"), 32)
            for n in range(3):
                m = dve.tensor_scalar(wnow[:, n, :], wproj[:, n, :], par[:, 2 + n:3 + n], None, ALU.mult)
            m.then_inc(S("wnow_ready"), 1)
            dve.wait_ge(S("edecay_ready"), 1)
            dve.tensor_scalar(wdecay[:], edecay[:], -1.0, None, ALU.mult).then_inc(S("wdecay_ready"), 1)
            dve.wait_ge(S("wnow_ready"), 1)
            dve.tensor_tensor(wprev[:], wproj[:, 0:3, :], wnow[:], ALU.subtract).then_inc(S("proj_ready"), 1)
            dve.wait_ge(S("edges_ready"), 1)
            dve.wait_ge(S("wdecay_ready"), 1)
            dve.wait_ge(S("tables"), 7)

            def decay_args(c):
                dve.wait_ge(S("k_ready"), c + 1)
                for s in range(SEQS):
                    m = dve.tensor_tensor_scan(pmax[:, s, 1:], wdecay[:, 0:1].to_broadcast([P, T]),
                                               pK[:, s * T:(s + 1) * T], NEG, ALU.add, ALU.max)
                m.then_inc(S("pmax_ready"), 1)
                dve.wait_ge(S("pmax_ready"), c + 1)
                dve.tensor_tensor(seq2(z[:]), seq2(pK[:]), pmax[:, :, 0:T], ALU.subtract).then_inc(S("z_ready"), 1)
                dve.wait_ge(S("z_ready"), c + 1)
                dve.tensor_scalar(arg[:, 0, :], z[:], edecay[:, 0:1], 0.0, ALU.add, ALU.max)
                dve.tensor_scalar(arg[:, 1, :], z[:], par[:, 1:2], 0.0, ALU.add, ALU.max).then_inc(S("args_ready"), 1)
                dve.tensor_scalar(arg[:, 2, :], z[:], edecay[:, 0:1], 0.0, ALU.add, ALU.min)
                dve.tensor_scalar(arg[:, 3, :], z[:], par[:, 1:2], 0.0, ALU.add, ALU.min).then_inc(S("args_ready"), 1)

            def recur(c):
                dve.wait_ge(S("facs_ready"), c * 2 + 2)
                dve.wait_ge(S("v_ready"), c + 1)
                dve.tensor_tensor(fv[:], f2, pV[:], ALU.mult).then_inc(S("fv_ready"), 1)
                dve.tensor_tensor_scan(sb_[:, 1:], f1, f2, 0.0, ALU.mult, ALU.add).then_inc(S("b_ready"), 1)
                dve.wait_ge(S("fv_ready"), c + 1)
                dve.tensor_tensor_scan(sa_[:, 1:], f1, fv[:], 0.0, ALU.mult, ALU.add).then_inc(S("a_ready"), 1)
                dve.tensor_tensor(ev[:], e2, pV[:], ALU.mult).then_inc(S("vprods_ready"), 1)
                dve.wait_ge(S("b_ready"), c + 1)
                dve.tensor_tensor(den0[:], e1, sb_[:, 0:CHUNK], ALU.mult).then_inc(S("den0_ready"), 1)
                dve.wait_ge(S("a_ready"), c + 1)
                dve.tensor_tensor(num0[:], e1, sa_[:, 0:CHUNK], ALU.mult).then_inc(S("num0_ready"), 1)
                dve.wait_ge(S("den0_ready"), c + 1)
                dve.tensor_tensor(den1[:], den0[:], e2, ALU.add).then_inc(S("den1_ready"), 1)
                dve.wait_ge(S("num0_ready"), c + 1)
                dve.wait_ge(S("vprods_ready"), c + 1)
                dve.tensor_tensor(num[:], num0[:], ev[:], ALU.add).then_inc(S("num_ready"), 1)
                dve.wait_ge(S("den1_ready"), c + 1)
                dve.wait_ge(S("rexp_ready"), c + 1)
                dve.scalar_tensor_tensor(den[:], rexp[:], 1.0, den1[:], ALU.add, ALU.mult).then_inc(S("den_ready"), 1)

            ROUTE = 18

            def route(q, c1):
                n = [0]

                def link(m):
                    n[0] += 1
                    m.then_inc(S("route_step"), 1)
                    dve.wait_ge(S("route_step"), q * ROUTE + n[0])

                L1, L2 = LL[:, 0], LL[:, 1]

                def choose(g):
                    link(dve.tensor_reduce(top[:, g, :], LL[:, g], AX_X, ALU.max))
                    link(dve.tensor_tensor(eq[:, g], LL[:, g], bc(top[:, g, :], 2, E), ALU.is_equal))
                    link(dve.tensor_tensor(pick[:, g], eq[:, g], bc(prio[:], 1, PAIRT), ALU.mult))
                    link(dve.tensor_reduce(pbest[:, g, :], pick[:, g], AX_X, ALU.max))
                    link(dve.tensor_tensor(hot[:, g], pick[:, g], bc(pbest[:, g, :], 2, E), ALU.is_equal))

                choose(0)
                link(dve.scalar_tensor_tensor(L2, hot[:, 0], DROP, L1, ALU.mult, ALU.add))
                choose(1)
                dve.tensor_tensor(hots[:], hot[:, 0], hot[:, 1], ALU.add).then_inc(S("hots_ready"), 1)
                flat = lambda t: t[:].rearrange("p g t e -> p (g t) e")
                topb = bc(top[:].rearrange("p g t -> p (g t)"), 2, E)
                dve.tensor_tensor(flat(dif), flat(LL), topb, ALU.subtract).then_inc(S("dif_ready"), 1)
                link(dve.scalar_tensor_tensor(flat(mag), flat(LL), -1.0, flat(LL), ALU.mult, ALU.max))
                link(dve.tensor_tensor(flat(lim), flat(mag), topb, ALU.max))
                dve.wait_ge(S("dif_ready"), q + 1)
                link(dve.scalar_tensor_tensor(flat(keep), flat(lim), -JITTER2, flat(dif), ALU.mult, ALU.is_le))
                dve.wait_ge(S("dexp_ready"), q + 1)
                link(dve.tensor_tensor(kexp[:], keep[:], dexp[:], ALU.mult))
                link(dve.tensor_reduce(ksum[:], kexp[:], AX_X, ALU.add))
                for h in range(2):
                    dve.wait_ge(S(f"dest_ready{h}"), q + 1)
                for h in range(2):
                    dve.reciprocal(hrow[:, h, :, :, C + 1], ksum[:, :, h * TILES:(h + 1) * TILES])
                dve.wait_ge(S("ranks_ready"), q + 1)
                link(dve.tensor_tensor(pos[:], pRank.rearrange("p (t e) -> p t e", e=E), bc(base[:], 1, PAIRT),
                                       ALU.add))
                dve.tensor_tensor(base[:], base[:], pCount, ALU.add).then_inc(S("ranks_read"), 1)
                link(dve.tensor_tensor(hpos[:], hot[:], bc(pos[:], 1, 2), ALU.mult))
                with nc.allow_low_precision(reason="row numbers are whole and under 2**24"):
                    dve.tensor_reduce(slot[:], hpos[:], AX_X, ALU.add).then_inc(S("slots_ready"), 1)
                dve.wait_ge(S("ranks_read"), q + 1)
                assert n[0] == ROUTE

            def step(c, parity):
                is0 = isinstance(c, int) and c == 0
                last = isinstance(c, int) and c >= NCH - 1
                ends = isinstance(c, int) and c == NCH
                if not last:
                    stats1(c + 1)
                if not is0:
                    dve.wait_ge(S("attn_ready"), c)
                    xc = xs[:, bass.ds((c - 1) * TILES, TILES), :]
                    dve.tensor_tensor(xc, xc, til(pAttn[:]), ALU.add).then_inc(S("x1_ready"), 1)
                    dve.wait_ge(S("x1_ready"), c)
                    settle(dve)
                    stats2(c - 1)
                if not ends:
                    decay_args(c)
                if not last:
                    norm1(c + 1)
                if not is0:
                    norm2(c - 1)
                if not ends:
                    recur(c)
                    dve.wait_ge(S("lden_ready"), c + 1)
                    dve.scalar_tensor_tensor(garg[:], pR[:], 0.0, lden[:], ALU.min, ALU.subtract)\
                        .then_inc(S("garg_ready"), 1)
                if not is0:
                    half = (parity + 1) % 2
                    dve.wait_ge(S("logits_ready"), c)
                    dve.tensor_copy(LL[:, 0, half * TILES:(half + 1) * TILES, :],
                                    pLogit.rearrange("p (t e) -> p t e", e=E)).then_inc(S("logits_read"), 1)
                    dve.wait_ge(S("logits_read"), c)
                if not ends:
                    dve.wait_ge(S("gfac_ready"), c + 1)
                    if not is0:
                        dve.wait_ge(S("attn_ready"), c)
                    dve.tensor_tensor(yT[:], num[:], gfac[:], ALU.mult).then_inc(S("yT_ready"), 1)
                if parity == 0 and not is0:
                    route(c // 2 - 1 if isinstance(c, int) else step.pairs, c)

            step(0, 0)
            dve.wait_ge(S("x_rest"), 16)
            with dve.Fori(0, (NCH - 2) // 2, 1) as i:
                step.pairs = i
                step(i * 2 + 1, 1)
                step(i * 2 + 2, 0)
            step(NCH - 1, 1)
            step(NCH, 0)

            made = [0]

            def link(m):
                made[0] += 1
                m.then_inc(S("plan_step"), 1)
                dve.wait_ge(S("plan_step"), made[0])

            dve.tensor_scalar(padidx[:], base[:], pcol[:, 0:1], None, ALU.add).then_inc(S("pads_ready"), 1)
            link(dve.tensor_tensor(cnt[:], base[:], ereg[:], ALU.subtract))
            link(dve.tensor_tensor(more[:], bc(cnt[:], 2, TOKENS // P), bc(thr[:], 1, E), ALU.is_gt))
            link(dve.tensor_reduce(ntile[:], more[:], AX_X, ALU.add))
            link(dve.tensor_tensor_scan(tend[:], ones8[:], ntile[:], 0.0, ALU.mult, ALU.add))
            link(dve.tensor_tensor(tstart[:], tend[:], ntile[:], ALU.subtract))
            link(dve.tensor_scalar(started[:], tstart[:], pcol[:, 0:1], None, ALU.is_le))
            link(dve.tensor_scalar(ended[:], tend[:], pcol[:, 0:1], None, ALU.is_le))
            link(dve.tensor_tensor(inside[:], started[:], ended[:], ALU.subtract))
            link(dve.scalar_tensor_tensor(rbase[:], tstart[:], -float(P), ereg[:], ALU.mult, ALU.add))
            link(dve.tensor_scalar(rowv[:], rbase[:], pcol[:, 1:2], None, ALU.add))
            link(dve.tensor_tensor(prod[:, 0, :], inside[:], rowv[:], ALU.mult))
            link(dve.tensor_tensor(prod[:, 1, :], inside[:], eoff[:], ALU.mult))
            link(dve.tensor_reduce(sums[:], prod[:], AX_X, ALU.add))
            dve.tensor_copy(plan[:, 1:2], sums[:, 1:2])
            dve.scalar_tensor_tensor(plan[:, 0:1], ended[:, E - 1:E], float(DUMMY), sums[:, 0:1],
                                     ALU.mult, ALU.add).then_inc(S("plan_ready"), 1)
            dve.wait_ge(S("planT_ready"), 1)
            dve.tensor_copy(table[:].rearrange("p n t -> p (n t)"), pSmall[0:1, 256:256 + 2 * NT])\
                .then_inc(S("table_ready"), 1)

            def hidden(j, b, first=False):
                dve.wait_ge(S("silu_ready"), j + 1)
                dve.wait_ge(S("up_ready"), j + 1)
                if not first:
                    dve.wait_ge(S("h_turned"), j - 1)
                dve.tensor_tensor(hh[b % 2][:], sg[b % 2][:], pUp[b % 2][:], ALU.mult).then_inc(S("h_ready"), 1)

            def take_h(j, b, first=False):
                dve.wait_ge(S("h_turned"), j + 1)
                if not first:
                    dve.wait_ge(S("down_ready"), j - 1)
                dve.tensor_copy(hhT[b % 2][:], pHt[b % 2][:]).then_inc(S("hT_done"), 1)

            hidden(0, 0, first=True)
            for j in range(1, RING):
                hidden(j, j, first=j < 2)
                take_h(j - 1, j - 1, first=j < 3)
            with dve.Fori(0, NT // RING - 1, 1) as i:
                for u in range(RING):
                    hidden(i * RING + (RING + u), u)
                    take_h(i * RING + (RING + u - 1), (u + RING - 1) % RING)
            take_h(NT - 1, NT - 1)

            for c in range(NCH):
                ks = slice(c * TILES, (c + 1) * TILES)
                b = c % 2
                dve.wait_ge(S(f"y_loaded{c}"), 32)
                dve.tensor_tensor(fsum[:, b], ych[0][:, ks, :], ych[1][:, ks, :], ALU.add).then_inc(S("fsum"), 1)
                dve.wait_ge(S("fsum"), c + 1)
                gb = bc(gates[:, c * SEQS:(c + 1) * SEQS, 1, :], 2, TILES // SEQS)
                dve.tensor_tensor(fgat[:, b].rearrange("p (s k) c -> p s k c", s=SEQS),
                                  fsum[:, b].rearrange("p (s k) c -> p s k c", s=SEQS), gb, ALU.mult)\
                    .then_inc(S("fgat"), 1)
                dve.wait_ge(S("fgat"), c + 1)
                dve.tensor_tensor(xs[:, ks, :], xs[:, ks, :], fgat[:, b], ALU.add).then_inc(S("out_ready"), 1)


def kernel(L0_attn_x, L0_attn_time_decay, L0_attn_time_first, L0_attn_time_mix_k, L0_attn_time_mix_v,
           L0_attn_time_mix_r, L0_attn_Wk, L0_attn_Wv, L0_attn_Wr, L0_attn_Wo, L0_ffn_gate_w, L0_ffn_w1,
           L0_ffn_w2, L0_ffn_w3, L0_c, L0_wmod):
    import numpy as np
    import concourse.bacc as bacc
    from concourse.bass_utils import run_bass_kernel_spmd

    a = np.asarray
    arrays = {
        "x": a(L0_attn_x),
        "par": np.stack([a(v).reshape(-1) for v in (L0_attn_time_decay, L0_attn_time_first, L0_attn_time_mix_k,
                                                    L0_attn_time_mix_v, L0_attn_time_mix_r)], 1),
        "wproj": np.stack([a(w).T for w in (L0_attn_Wk, L0_attn_Wv, L0_attn_Wr, L0_attn_Wo)], 1),
        "gatew": a(L0_ffn_gate_w).T,
        "w1": a(L0_ffn_w1).transpose(2, 0, 1).reshape(P, E * F),
        "w3": a(L0_ffn_w3).transpose(2, 0, 1).reshape(P, E * F),
        "w2": a(L0_ffn_w2).reshape(E, C, FB, P).transpose(3, 0, 2, 1).reshape(P, E * F),
        "cT": a(L0_c).T,
        "wmod": a(L0_wmod),
    }
    arrays = {k: np.ascontiguousarray(v) for k, v in arrays.items()}
    nc = bacc.Bacc("TRN2", target_bir_lowering=False, num_devices=1)
    aps = [nc.dram_tensor("in_" + k, v.shape, mybir.dt.from_np(v.dtype), kind="ExternalInput").ap()
           for k, v in arrays.items()]
    out = nc.dram_tensor("out", (B, T, C), F32, kind="ExternalOutput").ap()
    block_program(nc, *aps, out)
    r = run_bass_kernel_spmd(nc, [{"in_" + k: v for k, v in arrays.items()}], core_ids=[0])
    return r.results[0]["out"]
```

```python
from contextlib import ExitStack

import concourse.bass as bass
from concourse import mybir

F32 = mybir.dt.float32
F32R = mybir.dt.float32r
BF16 = mybir.dt.bfloat16
I32 = mybir.dt.int32
U32 = mybir.dt.uint32
ALU = mybir.AluOpType
ACT = mybir.ActivationFunctionType
AX_X = mybir.AxisListType.X

P = 128
B, T, C = 16, 256, 128
TOKENS = B * T
E, F = 8, 512
FB = F // P
CHUNK = 512
SEQS = CHUNK // T
TILES = CHUNK // P
NCH = TOKENS // CHUNK
PAIRT = 2 * TILES
REGION = TOKENS + P
DUMMY = E * REGION
ROW = C + 2
NT = 72
RING = 8
PAIR_DMAS = 16 * 2 * PAIRT
NEG = -1e38
DROP = -3e38
NOWHERE = 1 << 20
EPS = 1e-5
JITTER2 = 0.02
assert (2 * TOKENS + E * (P - 1)) // P <= NT and NT % RING == 0


def bc(ap, axis, n):
    u = ap.unsqueeze(axis)
    shape = list(u.shape)
    shape[axis] = n
    return u.to_broadcast(shape)


def block_program(nc, x_d, par_d, wproj_d, gatew_d, w1_d, w3_d, w2_d, cT_d, wmod_d, out_d):
    with ExitStack() as ctx:
        def sb(name, shape, dt=F32):
            return ctx.enter_context(nc.sbuf_tensor(name, shape, dt))

        sems = {}

        def S(name):
            if name not in sems:
                sems[name] = ctx.enter_context(nc.semaphore(name))
            return sems[name]

        rows_d = nc.dram_tensor("expert_rows", [DUMMY + P, ROW], F32, kind="Internal").ap()
        y_d = nc.dram_tensor("choice_rows", [2 * TOKENS, C], F32, kind="Internal").ap()
        gates_d = nc.dram_tensor("gate_scratch", [B, 2 * C], F32, kind="Internal").ap()

        bank = [ctx.enter_context(nc.psum_tensor(f"bank{i}", [P, 512], F32)) for i in range(8)]
        pK, pV, pR, pXn, pXn2, pBack, pAttn, pSmall = bank
        pGate, pUp, pHt, pXt, pY = bank[0:2], bank[2:4], bank[4:6], bank[6], bank[7]
        pLogit = pSmall[:, 0:TILES * E]
        pRank = pAttn[:, 0:PAIRT * E]
        pCount = pAttn[:, 128:128 + E]

        ident = sb("ident", [P, P])
        before = sb("before", [P, P], BF16)
        ones = sb("ones", [P, P], BF16)
        ones8 = sb("ones8", [P, E])
        eps = sb("eps", [P, 1])
        par = sb("par", [P, 5])
        wproj = sb("wproj", [P, 4, C])
        wnow = sb("wnow", [P, 3, C])
        wprev = sb("wprev", [P, 3, C])
        gatew = sb("gatew", [P, E])
        w1 = sb("w1", [P, E * F])
        w3 = sb("w3", [P, E * F])
        w2 = sb("w2", [P, E * F])
        cT = sb("cT", [P, B])
        cexp = sb("cexp", [P, B])
        cinv = sb("cinv", [P, B])
        csilu = sb("csilu", [P, B])
        wmod = sb("wmod", [P, 6 * C])
        mods = sb("mods", [P, 4, B])
        gsign = sb("gsign", [B, 2 * C])
        gabs = sb("gabs", [B, 2 * C])
        graw = sb("graw", [B, 2 * C])
        gone = sb("gone", [B, 2 * C])
        gfix = sb("gfix", [B, 2 * C])
        gates = sb("gates", [P, B, 2, C])
        wog = sb("wog", [P, B, C])
        edecay = sb("edecay", [P, 1])
        wdecay = sb("wdecay", [P, 1])
        first_neg = sb("first_neg", [P, 1])
        prio = sb("prio", [P, E])
        ereg = sb("ereg", [P, E])
        eoff = sb("eoff", [P, E])
        thr = sb("thr", [P, TOKENS // P])
        pcol = sb("pcol", [P, 2])
        ids = sb("ids", [P, 2, TOKENS // P], I32)
        padrow = sb("padrow", [P, ROW])

        arena = sb("arena", [P, 16 * CHUNK + 2])
        taken = [0]

        def carve(*shape):
            n = 1
            for d in shape:
                n *= d
            piece = arena[:, taken[0]:taken[0] + n]
            taken[0] += n
            if len(shape) == 3:
                return piece.rearrange("p (a b c) -> p a b c", a=shape[0], b=shape[1])
            if len(shape) == 2:
                return piece.rearrange("p (a b) -> p a b", a=shape[0])
            return piece

        w1h, w3h = arena[:, 0:E * F], arena[:, E * F:2 * E * F]

        xs = sb("xs", [P, TOKENS // P, C])
        bn1 = sb("bn1", [P, TILES, 6])
        mv1 = sb("mv1", [P, TILES, 2])
        lnv1 = sb("lnv1", [P, TILES])
        rstd1 = sb("rstd1", [P, TILES])
        shift1 = sb("shift1", [P, TILES])
        bn2 = sb("bn2", [P, TILES, 6])
        mv2 = sb("mv2", [P, TILES, 2])
        lnv2 = sb("lnv2", [P, TILES])
        rstd2 = sb("rstd2", [P, TILES])
        xn = sb("xn", [P, TILES, C])
        xn2 = sb("xn2", [P, TILES, C])
        hT = sb("hT", [P, 2, SEQS, T + 1])
        h2T = sb("h2T", [P, CHUNK])
        pmax = sb("pmax", [P, SEQS, T + 1])
        z = carve(CHUNK)
        fac = carve(2, 5, CHUNK)
        fv = carve(CHUNK)
        state = carve(2, CHUNK + 1)
        mean = carve(2, CHUNK)
        rabs = sb("rabs", [P, CHUNK])
        rexp = sb("rexp", [P, CHUNK])
        lden = sb("lden", [P, CHUNK])
        garg = sb("garg", [P, CHUNK])
        gfac = sb("gfac", [P, CHUNK])
        yT = sb("yT", [P, CHUNK])
        hrow = sb("hrow", [P, 2, 2, 2, TILES, ROW])

        LL = sb("LL", [P, 2, PAIRT, E])
        top = sb("top", [P, 2, PAIRT])
        eq = sb("eq", [P, 2, PAIRT, E])
        pick = sb("pick", [P, 2, PAIRT, E])
        pbest = sb("pbest", [P, 2, PAIRT])
        hot = sb("hot", [P, 2, PAIRT, E])
        hots = sb("hots", [P, PAIRT, E], BF16)
        dif = sb("dif", [P, 2, PAIRT, E])
        mag = sb("mag", [P, 2, PAIRT, E])
        lim = sb("lim", [P, 2, PAIRT, E])
        keep = sb("keep", [P, 2, PAIRT, E])
        dexp = sb("dexp", [P, 2, PAIRT, E])
        kexp = sb("kexp", [P, 2, PAIRT, E])
        ksum = sb("ksum", [P, 2, PAIRT])
        base = sb("base", [P, E])
        pos = sb("pos", [P, PAIRT, E])
        hpos = sb("hpos", [P, 2, PAIRT, E])
        slot = sb("slot", [P, 2, PAIRT], I32)
        slot_last = sb("slot_last", [P, 2, PAIRT], I32)
        ends_row = sb("ends_row", [1, E], I32)

        cnt = sb("cnt", [P, E])
        more = sb("more", [P, E, TOKENS // P])
        ntile = sb("ntile", [P, E])
        tend = sb("tend", [P, E])
        tstart = sb("tstart", [P, E])
        started = sb("started", [P, E])
        ended = sb("ended", [P, E])
        inside = sb("inside", [P, E])
        rbase = sb("rbase", [P, E])
        rowv = sb("rowv", [P, E])
        prod = sb("prod", [P, 2, E])
        sums = sb("sums", [P, 2])
        plan = sb("plan", [P, 2])
        table = sb("table", [1, 2, NT], I32)

        X = [sb(f"X{i}", [P, ROW]) for i in range(RING)]
        xTh = [sb(f"xTh{i}", [P, P]) for i in range(2)]
        xTl = [sb(f"xTl{i}", [P, P]) for i in range(2)]
        sg = [sb(f"sg{i}", [P, F]) for i in range(2)]
        hh = [sb(f"hh{i}", [P, F]) for i in range(2)]
        hhT = [sb(f"hhT{i}", [P, F]) for i in range(2)]
        yy = [sb(f"yy{i}", [P, C]) for i in range(RING)]
        ych = [w[:].rearrange("p (k c) -> p k c", c=C) for w in (w1, w3)]

        seq2 = lambda ap: ap.rearrange("p (s t) -> p s t", s=SEQS)
        til = lambda ap: ap.rearrange("p (k c) -> p k c", k=TILES)

        def settle(eng):
            eng.sem_inc(S(f"settled_{eng.engine.name}"), 1)

        block = ctx.enter_context(nc.Block())

        def front(step):
            step.loop = 0
            for c in range(2):
                step(c)
            with step.engine.Fori(0, (NCH - 4) // 2, 1) as i:
                step.loop = i
                step(i * 2 + 2)
                step(i * 2 + 3, odd=True)
            for c in range(NCH - 2, NCH + 1):
                step(c, odd=c == NCH - 1)

        def step_kind(c):
            flat = isinstance(c, int)
            return flat and c == 0, not flat or c < NCH - 1, not flat or c < NCH - 2, not flat or c < NCH

        SINGLE = NCH // 2 - 2
        ROUNDS = SINGLE + 4

        def window(r):
            if isinstance(r, int) and r >= SINGLE:
                half = (r - SINGLE) % 2
                return slice(half * TILES, (half + 1) * TILES)
            return slice(0, PAIRT)

        def pair_of(r):
            return r if r < SINGLE else SINGLE + (r - SINGLE) // 2

        def par_of(c, odd):
            return c % 2 if isinstance(c, int) else int(odd)

        def round_of(c, loop, odd):
            if isinstance(c, int):
                return None if c < 3 else c - (NCH - 2) + SINGLE
            return loop if odd else None

        @block.sync
        def _(sp):
            xv = x_d.rearrange("b (h p) c -> p (b h) c", p=P)
            cut = 2 * TILES
            sp.dma_start(xs[:, 0:cut, :], xv[:, 0:cut, :]).then_inc(S("x_head"), 16)
            sp.dma_start(cT[:], cT_d).then_inc(S("cond_loaded"), 16)
            sp.dma_start(wmod[:], wmod_d).then_inc(S("cond_loaded"), 16)
            sp.dma_start(par[:], par_d).then_inc(S("par_loaded"), 16)
            sp.dma_start(wproj[:], wproj_d).then_inc(S("par_loaded"), 16)
            sp.dma_start(xs[:, cut:, :], xv[:, cut:, :]).then_inc(S("x_rest"), 16)
            sp.dma_start(gatew[:], gatew_d).then_inc(S("gatew_loaded"), 16)
            sp.wait_ge(S("gfix_ready"), 1)
            sp.dma_start(gates_d, gfix[:]).then_inc(S("gates_stored"), 16)
            sp.wait_ge(S("gates_stored"), 16)
            sp.dma_start(gates[:].rearrange("p b g c -> p (b g c)"),
                         gates_d.rearrange("b g -> (b g)").partition_broadcast(P)).then_inc(S("gates_loaded"), 16)
            sp.wait_ge(S("padrow_ready"), 2)
            sp.dma_start(rows_d[DUMMY:DUMMY + P, :], padrow[:]).then_inc(S("dummy_stored"), 16)
            sp.dma_start(w1[:], w1_d).then_inc(S("experts_loaded"), 16)
            sp.dma_start(w3[:], w3_d).then_inc(S("experts_loaded"), 16)
            sp.dma_start(w2[:], w2_d).then_inc(S("experts_loaded"), 16)

            sp.wait_ge(S("ends_ready"), 1)
            for e in range(E):
                row = sp.value_load(ends_row[0:1, e:e + 1], min_val=e * REGION, max_val=e * REGION + TOKENS)
                sp.dma_start(rows_d[bass.ds(row, P), :], padrow[:]).then_inc(S("pads_landed"), 16)

            sp.wait_ge(S("dummy_stored"), 16)
            sp.wait_ge(S("pads_landed"), 16 * E)
            sp.wait_ge(S("rows_landed"), PAIR_DMAS * NCH // 2)
            sp.wait_ge(S("table_ready"), 1)

            def load_tile(j, b):
                row = sp.value_load(table[0:1, 0, bass.ds(j, 1)], min_val=0, max_val=DUMMY)
                sp.dma_start(X[b][:], rows_d[bass.ds(row, P), :]).then_inc(S(f"tile_loaded{b}"), 16)

            for b in range(RING):
                load_tile(b, b)
            with sp.Fori(1, NT // RING, 1) as i:
                for b in range(RING):
                    sp.wait_ge(S(f"y_landed{b}"), i * 16)
                    load_tile(i * RING + b, b)

            for b in range(RING):
                sp.wait_ge(S(f"y_landed{b}"), 16 * NT // RING)
            yv = y_d.rearrange("(g k p) c -> p g k c", g=2, p=P)
            for c in range(NCH):
                for g in range(2):
                    sp.dma_start(ych[g][:, c * TILES:(c + 1) * TILES, :],
                                 yv[:, g, c * TILES:(c + 1) * TILES, :]).then_inc(S(f"y_loaded{c}"), 16)
            ov = out_d.rearrange("b (h p) c -> p (b h) c", p=P)
            for c in range(NCH):
                sp.wait_ge(S("out_ready"), c + 1)
                sp.dma_start(ov[:, c * TILES:(c + 1) * TILES, :],
                             xs[:, c * TILES:(c + 1) * TILES, :]).then_inc(S("out_stored"), 16)
            sp.wait_ge(S("out_stored"), 16 * NCH)

        @block.gpsimd
        def _(pool):
            pool.memset(ident[:], 0.0).then_inc(S("blank"), 1)
            pool.memset(before[:], 1.0).then_inc(S("blank"), 1)
            pool.memset(ones[:], 1.0).then_inc(S("ones_ready"), 1)
            pool.wait_ge(S("blank"), 2)
            pool.affine_select(out=ident[:], in_=ident[:], compare_op=ALU.not_equal, fill=1.0, base=0,
                               pattern=[[-1, P]], channel_multiplier=1).then_inc(S("ident_ready"), 1)
            pool.affine_select(out=before[:], in_=before[:], compare_op=ALU.is_gt, fill=0.0, base=0,
                               pattern=[[1, P]], channel_multiplier=-1).then_inc(S("before_ready"), 1)
            fl = dict(allow_small_or_imprecise_dtypes=True)
            pool.iota(prio[:], [[-1, E]], base=E, channel_multiplier=0, **fl).then_inc(S("tables"), 1)
            pool.iota(ereg[:], [[REGION, E]], base=0, channel_multiplier=0, **fl).then_inc(S("tables"), 1)
            pool.iota(eoff[:], [[F, E]], base=0, channel_multiplier=0, **fl).then_inc(S("tables"), 1)
            pool.iota(base[:], [[REGION, E]], base=0, channel_multiplier=0, **fl).then_inc(S("tables"), 1)
            pool.iota(thr[:], [[P, TOKENS // P]], base=0, channel_multiplier=0, **fl).then_inc(S("tables"), 1)
            pool.iota(pcol[:, 0:1], [[0, 1]], base=0, channel_multiplier=1, **fl).then_inc(S("tables"), 1)
            pool.iota(pcol[:, 1:2], [[0, 1]], base=0, channel_multiplier=P, **fl).then_inc(S("tables"), 1)
            pool.iota(ids[:], [[TOKENS, 2], [P, TOKENS // P]], base=0, channel_multiplier=1).then_inc(S("ids_ready"), 1)
            pool.memset(padrow[:], 0.0).then_inc(S("padrow_ready"), 1)
            pool.wait_ge(S("padrow_ready"), 1)
            pool.iota(padrow[:, C:C + 1].bitcast(I32), [[0, 1]], base=NOWHERE, channel_multiplier=0)\
                .then_inc(S("padrow_ready"), 1)
            pool.wait_ge(S("gates_loaded"), 16)
            pool.wait_ge(S("par_loaded"), 32)
            pool.tensor_tensor(wog[:], bc(wproj[:, 3, :], 1, B), gates[:, :, 0, :], ALU.mult)\
                .then_inc(S("wog_ready"), 1)
            pool.wait_ge(S("ids_ready"), 1)

            def address(q):
                for h in range(2):
                    m = pool.tensor_copy(hrow[:, q % 2, h, :, :, C].bitcast(I32),
                                         ids[:, :, q * PAIRT + h * TILES:q * PAIRT + (h + 1) * TILES])
                m.then_inc(S("dest_ready"), 1)

            address(0)
            address(1)
            pool.wait_ge(S("dest_ready"), 2)
            for r in range(ROUNDS):
                pool.wait_ge(S("slots_ready"), r + 1)
                pool.wait_ge(S("rows_ready"), r * 2 + 2 if r < SINGLE else SINGLE + r + 1)
                q = pair_of(r)
                places = slot_last if q == NCH // 2 - 1 else slot
                w = window(r)
                for t in range(w.start, w.stop):
                    for g in range(2):
                        pool.indirect_dma_start(
                            rows_d, bass.IndirectOffsetOnAxis(ap=places[:, g, t:t + 1].bitcast(U32), axis=0),
                            hrow[:, q % 2, t // TILES, g, t % TILES, :], None).then_inc(S("rows_landed"), 16)
                if r < SINGLE:
                    pool.wait_ge(S("rows_landed"), PAIR_DMAS * (q + 1))
                    address(q + 2)
            with pool.Fori(0, NT // RING, 1) as i:
                for b in range(RING):
                    pool.wait_ge(S("y_ready"), i * RING + (b + 1))
                    settle(pool)
                    pool.indirect_dma_start(
                        y_d, bass.IndirectOffsetOnAxis(ap=X[b][:, C:C + 1].bitcast(U32), axis=0), yy[b][:], None,
                        bounds_check=2 * TOKENS - 1, oob_is_err=False).then_inc(S(f"y_landed{b}"), 16)

        @block.tensor
        def _(pe):
            pe.wait_ge(S("cond_loaded"), 32)
            pe.wait_ge(S("csilu_ready"), 1)
            for n, j in enumerate((0, 1, 3, 4)):
                pe.matmul(pAttn[:, n * B:(n + 1) * B], wmod[:, j * C:(j + 1) * C], csilu[:], start=True, stop=True)
            for n, j in enumerate((2, 5)):
                m = pe.matmul(pBack[0:B, n * C:(n + 1) * C], csilu[:], wmod[:, j * C:(j + 1) * C],
                              start=True, stop=True)
            m.then_inc(S("mods_ready"), 1)
            pe.wait_ge(S("ident_ready"), 1)

            def turn1(c, first=False):
                pe.wait_ge(S("xn_ready"), c + 1)
                if not first:
                    pe.wait_ge(S("hT_ready"), c)
                for k in range(TILES):
                    m = pe.transpose(pXn[:, k * P:(k + 1) * P], xn[:, k, :], ident[:])
                m.then_inc(S("xnT_ready"), 1)

            def project(n, buf, dst, done):
                pe.matmul(seq2(dst[:]), wnow[:, n, :], hT[:, buf, :, 1:], start=True, stop=False)
                pe.matmul(seq2(dst[:]), wprev[:, n, :], hT[:, buf, :, 0:T], start=False, stop=True).then_inc(S(done), 1)

            def proj_k(c, buf, first=False):
                pe.wait_ge(S("hT_ready"), c + 1)
                if not first:
                    pe.wait_ge(S("z_ready"), c)
                project(0, buf, pK, "k_ready")

            def proj_v(c, buf, first=False):
                if not first:
                    pe.wait_ge(S("vprods_ready"), c)
                project(1, buf, pV, "v_ready")

            def proj_r(c, buf, first=False):
                if not first:
                    pe.wait_ge(S("garg_ready"), c)
                project(2, buf, pR, "r_ready")

            def ranks(r):
                pe.wait_ge(S("hots_ready"), r + 1)
                w = window(r)
                n = w.stop - w.start
                hv = hots[:, w, :].rearrange("p t e -> p (t e)")
                pe.matmul(pRank[:, 0:n * E], before[:], hv, start=True, stop=False)
                for d in range(1, n):
                    m = pe.matmul(pRank[:, d * E:n * E], ones[:], hv[:, 0:(n - d) * E], start=False, stop=d == n - 1)
                for t in range(n):
                    m = pe.matmul(pCount, ones[:], hv[:, t * E:(t + 1) * E], start=t == 0, stop=t == n - 1)
                m.then_inc(S("ranks_ready"), 1)

            def step(c, odd=False):
                is0, has1, has2, has = step_kind(c)
                nxt = 1 - par_of(c, odd)
                if has1:
                    proj_k(c + 1, nxt)
                if not is0:
                    pe.wait_ge(S("xn2_ready"), c)
                    for k in range(TILES):
                        m = pe.transpose(pXn2[:, k * P:(k + 1) * P], xn2[:, k, :], ident[:])
                    m.then_inc(S("xn2T_ready"), 1)
                r = round_of(c, step.loop, odd)
                if r is not None:
                    ranks(r)
                if has1:
                    proj_v(c + 1, nxt)
                if not is0:
                    pe.wait_ge(S("h2T_ready"), c)
                    for k in range(TILES):
                        m = pe.matmul(pLogit[:, k * E:(k + 1) * E], h2T[:, k * P:(k + 1) * P], gatew[:],
                                      start=True, stop=True)
                    m.then_inc(S("logits_ready"), 1)
                    if not (isinstance(c, int) and c == 1):
                        pe.wait_ge(S("rows_ready"), c - 1)
                    for k in range(TILES):
                        m = pe.transpose(pBack[:, k * P:(k + 1) * P], h2T[:, k * P:(k + 1) * P], ident[:])
                    m.then_inc(S("back_ready"), 1)
                if has2:
                    turn1(c + 2)
                if has:
                    pe.wait_ge(S("yT_ready"), c + 1)
                    for k in range(TILES):
                        m = pe.matmul(pAttn[:, k * P:(k + 1) * P], yT[:, k * P:(k + 1) * P],
                                      wog[:, bass.ds(c * SEQS + k // (TILES // SEQS), 1), :],
                                      start=True, stop=True)
                    m.then_inc(S("attn_ready"), 1)
                if has1:
                    proj_r(c + 1, nxt)

            step.engine = pe
            pe.wait_ge(S("proj_ready"), 1)
            turn1(0, first=True)
            proj_k(0, 0, first=True)
            proj_v(0, 0, first=True)
            proj_r(0, 0, first=True)
            turn1(1)
            pe.wait_ge(S("gatew_loaded"), 16)
            pe.wait_ge(S("wog_ready"), 1)
            pe.wait_ge(S("before_ready"), 1)
            pe.wait_ge(S("ones_ready"), 1)
            front(step)

            ranks(ROUNDS - 1)

            pe.wait_ge(S("plan_ready"), 1)
            for n in range(2):
                m = pe.transpose(pSmall[0:1, 256 + n * NT:256 + (n + 1) * NT], plan[0:NT, n:n + 1], ident[0:NT, 0:NT])
            m.then_inc(S("planT_ready"), 1)

            pe.wait_ge(S("table_ready"), 1)
            pe.wait_ge(S("experts_loaded"), 48)
            pe.wait_ge(S("split_ready"), 2)

            def turn_x(j, b, u, first=False):
                pe.wait_ge(S(f"tile_loaded{b}"), u)
                if not first:
                    pe.wait_ge(S("xT_ready"), j)
                pe.transpose(pXt[:, 0:P], X[b][:, 0:C], ident[:]).then_inc(S("tile_turned"), 1)

            def weights_of(j):
                return pe.value_load(table[0:1, 1, bass.ds(j, 1)], min_val=0, max_val=(E - 1) * F)

            def gate_up(j, b, off, first=False):
                pe.wait_ge(S("xT_ready"), j + 1)
                if not first:
                    pe.wait_ge(S("h_ready"), j - 1)
                xh, xl = xTh[b % 2][:].bitcast(F32R), xTl[b % 2][:].bitcast(F32R)
                for dst, high, low, done in ((pGate, w1h, w1, "gate_ready"), (pUp, w3h, w3, "up_ready")):
                    wh, wl = (t[:, bass.ds(off, F)].bitcast(F32R) for t in (high, low))
                    pe.matmul(dst[b % 2][:], xh, wh, start=True, stop=False)
                    pe.matmul(dst[b % 2][:], xh, wl, start=False, stop=False)
                    pe.matmul(dst[b % 2][:], xl, wh, start=False, stop=True).then_inc(S(done), 1)

            def turn_h(j, b, first=False):
                pe.wait_ge(S("h_ready"), j + 1)
                if not first:
                    pe.wait_ge(S("hT_done"), j - 1)
                for k in range(FB):
                    m = pe.transpose(pHt[b % 2][:, k * P:(k + 1) * P], hh[b % 2][:, k * P:(k + 1) * P], ident[:])
                m.then_inc(S("h_turned"), 1)

            def down(j, b, off, first=False):
                pe.wait_ge(S("hT_done"), j + 1)
                if not first:
                    pe.wait_ge(S("y_ready"), j)
                for k in range(FB):
                    m = pe.matmul(pY[:, 0:C], hhT[b % 2][:, k * P:(k + 1) * P], w2[:, bass.ds(off + k * P, P)],
                                  start=k == 0, stop=k == FB - 1)
                m.then_inc(S("down_ready"), 1)

            def loads(j):
                return 16 * (j // RING + 1)

            def tile_step(s, b, offs, i=None):
                flat = isinstance(s, int)
                if not flat or s < NT:
                    gate_up(s, b, offs[0], first=flat and s < 2)
                if (not flat or s + 1 < NT) and b < RING - 1:
                    offs[1] = weights_of(s + 1)
                if not flat or s + 1 < NT:
                    turn_x(s + 1, (b + 1) % RING, loads(s + 1) if flat else i * 16 + 32 + 16 * ((b + 1) // RING))
                if not flat or 0 <= s - 1 < NT:
                    turn_h(s - 1, (b - 1) % RING, first=flat and s < 3)
                if not flat or s >= 2:
                    down(s - 2, (b - 2) % RING, offs[-2] if -2 in offs else weights_of(s - 2), first=flat and s < 3)
                return {k - 1: v for k, v in offs.items()}

            turn_x(0, 0, loads(0), first=True)
            offs = {0: weights_of(0)}
            for s in range(RING):
                offs = tile_step(s, s, offs)
            with pe.Fori(0, NT // RING - 2, 1) as i:
                offs = {0: weights_of(i * RING + RING)}
                for b in range(RING):
                    offs = tile_step(i * RING + (RING + b), b, offs, i)
            offs = {0: weights_of(NT - RING)}
            for s in range(NT - RING, NT + 2):
                offs = tile_step(s, s % RING, offs)

        @block.scalar
        def _(act):
            act.preload_act_table_set("natural_log_exp_and_others")
            act.wait_ge(S("cond_loaded"), 32)
            act.activation(cexp[:], cT[:], ACT.Exp, scale=-1.0).then_inc(S("cexp_ready"), 1)
            act.wait_ge(S("par_loaded"), 32)
            act.activation(edecay[:], par[:, 0:1], ACT.Exp).then_inc(S("edecay_ready"), 1)
            act.wait_ge(S("eps_ready"), 1)

            def inv_std(c, mv, lnv, rstd, moments, logged, ready):
                act.wait_ge(S(moments), c + 1)
                act.activation(lnv[:], mv[:, :, 1], ACT.Ln, bias=eps[:, 0:1]).then_inc(S(logged), 1)
                act.wait_ge(S(logged), c + 1)
                act.activation(rstd[:], lnv[:], ACT.Exp, scale=-0.5).then_inc(S(ready), 1)

            def std1(c):
                inv_std(c, mv1, lnv1, rstd1, "moments1_ready", "lnv1_ready", "rstd1_ready")

            def std2(c):
                inv_std(c, mv2, lnv2, rstd2, "moments2_ready", "lnv2_ready", "rstd2_ready")

            def norm(c, dst, rstd, shift, ready):
                for k in range(TILES):
                    m = act.activation(dst[:, k, :], xs[:, bass.ds(c * TILES + k, 1), :], ACT.Identity,
                                       scale=rstd[:, k:k + 1], bias=shift[:, k:k + 1])
                m.then_inc(S(ready), 1)

            def norm1(c):
                act.wait_ge(S("shift1_ready"), c + 1)
                norm(c, xn, rstd1, shift1, "xn_ready")

            def factors(c, buf, n):
                act.wait_ge(S("z_ready"), c + 1)
                plus, minus = ((edecay[:, 0:1], wdecay[:, 0:1]), (par[:, 1:2], first_neg[:, 0:1]))[n]
                pair = fac[:, buf, 2 * n:2 * n + 2, :]
                act.activation(pair[:, 0, :], z[:], ACT.Relu, bias=plus)
                act.activation(pair[:, 1, :], z[:], ACT.Relu, scale=-1.0, bias=minus).then_inc(S("args_ready"), 1)
                act.wait_ge(S("args_ready"), c * 2 + (n + 1))
                act.activation(pair, pair, ACT.Exp, scale=-1.0).then_inc(S("facs_ready"), 1)

            def modulate1(c, buf, first=False):
                act.wait_ge(S("xnT_ready"), c + 1)
                if not first:
                    act.wait_ge(S("r_ready"), c - 1)
                for s in range(SEQS):
                    m = act.activation(hT[:, buf, s, 1:], pXn[:, s * T:(s + 1) * T], ACT.Identity,
                                       scale=mods[:, 1, bass.ds(c * SEQS + s, 1)],
                                       bias=mods[:, 0, bass.ds(c * SEQS + s, 1)])
                m.then_inc(S("hT_ready"), 1)

            def modulate2(c):
                act.wait_ge(S("xn2T_ready"), c + 1)
                for s in range(SEQS):
                    m = act.activation(h2T[:, s * T:(s + 1) * T], pXn2[:, s * T:(s + 1) * T], ACT.Identity,
                                       scale=mods[:, 3, bass.ds(c * SEQS + s, 1)],
                                       bias=mods[:, 2, bass.ds(c * SEQS + s, 1)])
                m.then_inc(S("h2T_ready"), 1)

            def step(c, odd=False):
                is0, has1, has2, has = step_kind(c)
                buf = par_of(c, odd)
                if has2:
                    std1(c + 2)
                if not is0:
                    std2(c - 1)
                if has:
                    factors(c, buf, 1)
                if has2:
                    norm1(c + 2)
                if has:
                    act.wait_ge(S("r_ready"), c + 1)
                    act.activation(rabs[:], pR[:], ACT.Abs).then_inc(S("rabs_ready"), 1)
                    act.wait_ge(S("rabs_ready"), c + 1)
                    act.activation(rexp[:], rabs[:], ACT.Exp, scale=-1.0).then_inc(S("rexp_ready"), 1)
                if not is0:
                    modulate2(c - 1)
                r = round_of(c, step.loop, odd)
                if r is not None:
                    likely(r)
                if has:
                    act.wait_ge(S("den_ready"), c + 1)
                    act.activation(lden[:], mean[:, 0, :], ACT.Ln).then_inc(S("lden_ready"), 1)
                    act.wait_ge(S("garg_ready"), c + 1)
                    act.activation(gfac[:], garg[:], ACT.Exp).then_inc(S("gfac_ready"), 1)
                if has1:
                    factors(c + 1, 1 - buf, 0)
                if has2:
                    modulate1(c + 2, buf)
                if not is0:
                    flat = isinstance(c, int)
                    pair = (c - 1) // 2 if flat else step.loop + int(odd)
                    half = (c - 1) % 2 if flat else int(not odd)
                    parity = pair % 2 if flat else step.loop * -1 + 1 if odd else step.loop
                    act.wait_ge(S("back_ready"), c)
                    act.wait_ge(S("dest_ready"), pair + 1)
                    act.activation(hrow[:, bass.ds(parity, 1), half, :, :, 0:C].squeeze(1),
                                   bc(til(pBack[:]), 1, 2), ACT.Copy).then_inc(S("rows_ready"), 1)

            def likely(r):
                act.wait_ge(S("dif_ready"), r + 1)
                w = window(r)
                act.activation(dexp[:, :, w, :], dif[:, :, w, :], ACT.Exp).then_inc(S("dexp_ready"), 1)

            step.engine = act
            std1(0)
            norm1(0)
            act.wait_ge(S("mods_fixed"), 1)
            modulate1(0, 0, first=True)
            std1(1)
            norm1(1)
            modulate1(1, 1, first=True)
            act.wait_ge(S("edges_ready"), 1)
            factors(0, 0, 0)
            front(step)
            likely(ROUNDS - 1)
            act.wait_ge(S("x1_ready"), NCH)
            act.wait_ge(S("experts_loaded"), 48)
            for w, high in ((w1, w1h), (w3, w3h)):
                act.activation(high.bitcast(F32R), w[:], ACT.Copy).then_inc(S("high_ready"), 1)

            act.preload_act_table(ACT.Silu)

            def silu(j, b, first=False):
                act.wait_ge(S("gate_ready"), j + 1)
                if not first:
                    act.wait_ge(S("h_ready"), j - 1)
                act.activation(sg[b % 2][:], pGate[b % 2][:], ACT.Silu).then_inc(S("silu_ready"), 1)

            def weigh(j, b):
                act.wait_ge(S("down_ready"), j + 1)
                act.activation(yy[b][:], pY[:, 0:C], ACT.Copy, scale=X[b][:, C + 1:C + 2]).then_inc(S("y_ready"), 1)

            def tile_step(s, b):
                flat = isinstance(s, int)
                if not flat or s < NT:
                    silu(s, b, first=flat and s < 2)
                if not flat or s >= 2:
                    weigh(s - 2, (b - 2) % RING)

            for s in range(RING):
                tile_step(s, s)
            with act.Fori(0, NT // RING - 2, 1) as i:
                for b in range(RING):
                    tile_step(i * RING + (RING + b), b)
            for s in range(NT - RING, NT + 2):
                tile_step(s, s % RING)

        @block.vector
        def _(dve):
            dve.memset(eps[:], EPS).then_inc(S("eps_ready"), 1)
            dve.memset(hT[:, :, :, 0], 0.0)
            dve.memset(pmax[:, :, 0], NEG)
            dve.memset(state[:, :, 0], 0.0)
            dve.memset(ones8[:], 1.0).then_inc(S("edges_ready"), 1)
            dve.wait_ge(S("cexp_ready"), 1)
            dve.tensor_scalar_add(cinv[:], cexp[:], 1.0).then_inc(S("cond"), 1)
            dve.wait_ge(S("cond"), 1)
            dve.reciprocal(cinv[:], cinv[:]).then_inc(S("cond"), 1)
            dve.wait_ge(S("cond"), 2)
            dve.tensor_tensor(csilu[:], cT[:], cinv[:], ALU.mult).then_inc(S("csilu_ready"), 1)

            def stats(c, bn, mv, told, ready):
                for k in range(TILES):
                    m = dve.bn_stats(bn[:, k, :], xs[:, bass.ds(c * TILES + k, 1), :])
                m.then_inc(S(told), 1)
                dve.wait_ge(S(told), c + 1)
                settle(dve)
                for k in range(TILES):
                    m = dve.bn_aggr(mv[:, k, :], bn[:, k, :])
                m.then_inc(S(ready), 1)

            def stats1(c):
                stats(c, bn1, mv1, "stats1", "moments1_ready")

            def stats2(c):
                stats(c, bn2, mv2, "stats2", "moments2_ready")

            def shift(c, sh, mv, rstd, known, ready):
                dve.wait_ge(S(known), c + 1)
                dve.scalar_tensor_tensor(sh[:], mv[:, :, 0], -1.0, rstd[:], ALU.mult, ALU.mult)\
                    .then_inc(S(ready), 1)

            def shift1_(c, first=False):
                if not first:
                    dve.wait_ge(S("xn_ready"), c)
                shift(c, shift1, mv1, rstd1, "rstd1_ready", "shift1_ready")

            def norm2(c):
                dve.wait_ge(S("rstd2_ready"), c + 1)
                for k in range(TILES):
                    m = dve.tensor_scalar(xn2[:, k, :], xs[:, bass.ds(c * TILES + k, 1), :], mv2[:, k, 0:1],
                                          rstd2[:, k:k + 1], ALU.subtract, ALU.mult)
                m.then_inc(S("xn2_ready"), 1)

            dve.wait_ge(S("x_head"), 16)
            stats1(0)
            shift1_(0, first=True)
            dve.wait_ge(S("mods_ready"), 1)
            mp = pAttn[:, 0:4 * B].rearrange("p (m b) -> p m b", m=4)
            for m_, one in ((0, 0.0), (1, 1.0), (2, 0.0), (3, 1.0)):
                m = dve.tensor_scalar_add(mods[:, m_, :], mp[:, m_, :], one)
            m.then_inc(S("mods_fixed"), 1)
            gp = pBack[0:B, 0:2 * C]
            dve.tensor_scalar(gsign[:], gp, 0.0, 2.0, ALU.is_ge, ALU.mult).then_inc(S("gate_parts"), 1)
            dve.tensor_copy(graw[:], gp).then_inc(S("gate_parts"), 1)
            dve.wait_ge(S("gate_parts"), 2)
            dve.scalar_tensor_tensor(gabs[:], graw[:], -1.0, graw[:], ALU.mult, ALU.max).then_inc(S("gate_parts"), 1)
            dve.tensor_scalar_add(gone[:], gsign[:], -1.0).then_inc(S("gate_parts"), 1)
            dve.wait_ge(S("gate_parts"), 4)
            dve.scalar_tensor_tensor(gfix[:], gabs[:], 0.25, gone[:], ALU.max, ALU.mult).then_inc(S("gfix_ready"), 1)
            dve.wait_ge(S("par_loaded"), 32)
            for n in range(3):
                m = dve.tensor_scalar(wnow[:, n, :], wproj[:, n, :], par[:, 2 + n:3 + n], None, ALU.mult)
            m.then_inc(S("wnow_ready"), 1)
            dve.wait_ge(S("edecay_ready"), 1)
            dve.tensor_scalar(first_neg[:], par[:, 1:2], -1.0, None, ALU.mult).then_inc(S("wdecay_ready"), 1)
            dve.tensor_scalar(wdecay[:], edecay[:], -1.0, None, ALU.mult).then_inc(S("wdecay_ready"), 1)
            dve.wait_ge(S("wnow_ready"), 1)
            dve.tensor_tensor(wprev[:], wproj[:, 0:3, :], wnow[:], ALU.subtract).then_inc(S("proj_ready"), 1)
            stats1(1)
            shift1_(1)
            dve.wait_ge(S("edges_ready"), 1)
            dve.wait_ge(S("wdecay_ready"), 2)
            dve.wait_ge(S("tables"), 7)

            def decay_args(c):
                dve.wait_ge(S("k_ready"), c + 1)
                for s in range(SEQS):
                    m = dve.tensor_tensor_scan(pmax[:, s, 1:], wdecay[:, 0:1].to_broadcast([P, T]),
                                               pK[:, s * T:(s + 1) * T], NEG, ALU.add, ALU.max)
                m.then_inc(S("pmax_ready"), 1)
                dve.wait_ge(S("pmax_ready"), c + 1)
                dve.tensor_tensor(seq2(z[:]), seq2(pK[:]), pmax[:, :, 0:T], ALU.subtract).then_inc(S("z_ready"), 1)

            def states(c, buf):
                f1, f2 = fac[:, buf, 0, :], fac[:, buf, 1, :]
                dve.wait_ge(S("facs_ready"), c * 2 + 1)
                dve.wait_ge(S("v_ready"), c + 1)
                dve.tensor_tensor(fv[:], f2, pV[:], ALU.mult).then_inc(S("fv_ready"), 1)
                dve.tensor_tensor_scan(state[:, 0, 1:], f1, f2, 0.0, ALU.mult, ALU.add)
                dve.wait_ge(S("fv_ready"), c + 1)
                dve.tensor_tensor_scan(state[:, 1, 1:], f1, fv[:], 0.0, ALU.mult, ALU.add)\
                    .then_inc(S("states_ready"), 1)

            def means(c, buf):
                e1, e2, ev = (fac[:, buf, n, :] for n in range(2, 5))
                dve.wait_ge(S("facs_ready"), c * 2 + 2)
                dve.tensor_tensor(ev, e2, pV[:], ALU.mult).then_inc(S("vprods_ready"), 1)
                dve.wait_ge(S("states_ready"), c + 1)
                dve.tensor_tensor(mean[:], bc(e1, 1, 2), state[:, :, 0:CHUNK], ALU.mult).then_inc(S("old_ready"), 1)
                dve.wait_ge(S("vprods_ready"), c + 1)
                dve.wait_ge(S("old_ready"), c + 1)
                dve.tensor_tensor(mean[:], mean[:], fac[:, buf, 3:5, :], ALU.add).then_inc(S("mean_ready"), 1)
                dve.wait_ge(S("mean_ready"), c + 1)
                dve.wait_ge(S("rexp_ready"), c + 1)
                dve.scalar_tensor_tensor(mean[:, 0, :], rexp[:], 1.0, mean[:, 0, :], ALU.add, ALU.mult)\
                    .then_inc(S("den_ready"), 1)

            ROUTE = 17

            def route_link(r, at):
                n = [at]

                def link(m):
                    n[0] += 1
                    m.then_inc(S("route_step"), 1)
                    dve.wait_ge(S("route_step"), r * ROUTE + n[0])

                return link

            def choose(r, g):
                link = route_link(r, 5 * g)
                w = window(r)
                n = w.stop - w.start
                logit, best, pri, chosen = LL[:, g, w, :], top[:, g, w], pick[:, g, w, :], hot[:, g, w, :]
                if g:
                    link(dve.scalar_tensor_tensor(logit, hot[:, 0, w, :], DROP, LL[:, 0, w, :], ALU.mult, ALU.add))
                link(dve.tensor_reduce(best, logit, AX_X, ALU.max))
                link(dve.tensor_tensor(eq[:, g, w, :], logit, bc(best, 2, E), ALU.is_equal))
                link(dve.tensor_tensor(pri, eq[:, g, w, :], bc(prio[:], 1, n), ALU.mult))
                link(dve.tensor_reduce(pbest[:, g, w], pri, AX_X, ALU.max))
                link(dve.tensor_tensor(chosen, pri, bc(pbest[:, g, w], 2, E), ALU.is_equal))
                if not g:
                    return
                logits, d, lm, kp, mg = (t[:, :, w, :] for t in (LL, dif, lim, keep, mag))
                topb = bc(top[:, :, w], 3, E)
                dve.tensor_tensor(hots[:, w, :], hot[:, 0, w, :], hot[:, 1, w, :], ALU.add).then_inc(S("hots_ready"), 1)
                dve.tensor_tensor(d, logits, topb, ALU.subtract).then_inc(S("dif_ready"), 1)
                link(dve.scalar_tensor_tensor(mg, logits, -1.0, logits, ALU.mult, ALU.max))
                link(dve.tensor_tensor(lm, mg, topb, ALU.max))
                dve.wait_ge(S("dif_ready"), r + 1)
                link(dve.scalar_tensor_tensor(kp, lm, -JITTER2, d, ALU.mult, ALU.is_le))

            def place(r):
                link = route_link(r, 14)
                w = window(r)
                n = w.stop - w.start
                dve.wait_ge(S("ranks_ready"), r + 1)
                link(dve.tensor_tensor(pos[:, w, :], pRank[:, 0:n * E].rearrange("p (t e) -> p t e", e=E),
                                       bc(base[:], 1, n), ALU.add))
                dve.tensor_tensor(base[:], base[:], pCount, ALU.add).then_inc(S("ranks_read"), 1)
                dve.tensor_tensor(hpos[:, :, w, :], hot[:, :, w, :], bc(pos[:, w, :], 1, 2), ALU.mult)\
                    .then_inc(S("hpos_ready"), 1)

            def weigh(r):
                link = route_link(r, 15)
                w = window(r)
                flat = isinstance(r, int)
                last = flat and pair_of(r) == NCH // 2 - 1
                dve.wait_ge(S("dexp_ready"), r + 1)
                link(dve.tensor_tensor(kexp[:, :, w, :], keep[:, :, w, :], dexp[:, :, w, :], ALU.mult))
                link(dve.tensor_reduce(ksum[:, :, w], kexp[:, :, w, :], AX_X, ALU.add))
                dve.wait_ge(S("dest_ready"), r + 2 if not flat else min(r + 2, NCH // 2))
                settle(dve)
                parity = pair_of(r) % 2 if flat else r
                for h in range(w.start // TILES, w.stop // TILES):
                    dve.reciprocal(hrow[:, bass.ds(parity, 1), h, :, :, C + 1].squeeze(1),
                                   ksum[:, :, h * TILES:(h + 1) * TILES])
                dve.wait_ge(S("hpos_ready"), r + 1)
                with nc.allow_low_precision(reason="row numbers are whole and under 2**24"):
                    dve.tensor_reduce((slot_last if last else slot)[:, :, w], hpos[:, :, w, :], AX_X, ALU.add)\
                        .then_inc(S("slots_ready"), 1)
                dve.wait_ge(S("ranks_read"), r + 1)

            def step(c, odd=False):
                is0, has1, has2, has = step_kind(c)
                r = round_of(c, step.loop, odd)
                if is0:
                    dve.wait_ge(S("x_rest"), 16)
                if has2:
                    stats1(c + 2)
                if not is0:
                    dve.wait_ge(S("attn_ready"), c)
                    xc = xs[:, bass.ds((c - 1) * TILES, TILES), :]
                    dve.tensor_tensor(xc, xc, til(pAttn[:]), ALU.add).then_inc(S("x1_ready"), 1)
                    dve.wait_ge(S("x1_ready"), c)
                    settle(dve)
                    stats2(c - 1)
                if r is not None:
                    choose(r, 0)
                if has:
                    states(c, par_of(c, odd))
                if has2:
                    shift1_(c + 2)
                if not is0:
                    norm2(c - 1)
                if r is not None:
                    choose(r, 1)
                if has:
                    means(c, par_of(c, odd))
                if has1:
                    decay_args(c + 1)
                if r is not None:
                    place(r)
                if has:
                    dve.wait_ge(S("lden_ready"), c + 1)
                    dve.scalar_tensor_tensor(garg[:], pR[:], 0.0, lden[:], ALU.min, ALU.subtract)\
                        .then_inc(S("garg_ready"), 1)
                if not is0:
                    half = (c - 1) % 2 if isinstance(c, int) else int(not odd)
                    dve.wait_ge(S("logits_ready"), c)
                    dve.tensor_copy(LL[:, 0, half * TILES:(half + 1) * TILES, :],
                                    pLogit.rearrange("p (t e) -> p t e", e=E)).then_inc(S("logits_read"), 1)
                if r is not None:
                    weigh(r)
                if has:
                    dve.wait_ge(S("gfac_ready"), c + 1)
                    dve.tensor_tensor(yT[:], mean[:, 1, :], gfac[:], ALU.mult).then_inc(S("yT_ready"), 1)
                if not is0:
                    dve.wait_ge(S("logits_read"), c)

            step.engine = dve
            decay_args(0)
            front(step)
            for g in range(2):
                choose(ROUNDS - 1, g)
            place(ROUNDS - 1)
            weigh(ROUNDS - 1)

            made = [0]

            def link(m):
                made[0] += 1
                m.then_inc(S("plan_step"), 1)
                dve.wait_ge(S("plan_step"), made[0])

            dve.tensor_copy(ends_row[:], base[0:1, :]).then_inc(S("ends_ready"), 1)
            link(dve.tensor_tensor(cnt[:], base[:], ereg[:], ALU.subtract))
            link(dve.tensor_tensor(more[:], bc(cnt[:], 2, TOKENS // P), bc(thr[:], 1, E), ALU.is_gt))
            link(dve.tensor_reduce(ntile[:], more[:], AX_X, ALU.add))
            link(dve.tensor_tensor_scan(tend[:], ones8[:], ntile[:], 0.0, ALU.mult, ALU.add))
            link(dve.tensor_tensor(tstart[:], tend[:], ntile[:], ALU.subtract))
            link(dve.tensor_scalar(started[:], tstart[:], pcol[:, 0:1], None, ALU.is_le))
            link(dve.tensor_scalar(ended[:], tend[:], pcol[:, 0:1], None, ALU.is_le))
            link(dve.tensor_tensor(inside[:], started[:], ended[:], ALU.subtract))
            link(dve.scalar_tensor_tensor(rbase[:], tstart[:], -float(P), ereg[:], ALU.mult, ALU.add))
            link(dve.tensor_scalar(rowv[:], rbase[:], pcol[:, 1:2], None, ALU.add))
            link(dve.tensor_tensor(prod[:, 0, :], inside[:], rowv[:], ALU.mult))
            link(dve.tensor_tensor(prod[:, 1, :], inside[:], eoff[:], ALU.mult))
            link(dve.tensor_reduce(sums[:], prod[:], AX_X, ALU.add))
            dve.tensor_copy(plan[:, 1:2], sums[:, 1:2])
            dve.scalar_tensor_tensor(plan[:, 0:1], ended[:, E - 1:E], float(DUMMY), sums[:, 0:1],
                                     ALU.mult, ALU.add).then_inc(S("plan_ready"), 1)
            dve.wait_ge(S("planT_ready"), 1)
            dve.tensor_copy(table[:].rearrange("p n t -> p (n t)"), pSmall[0:1, 256:256 + 2 * NT])\
                .then_inc(S("table_ready"), 1)
            for n, (w, high) in enumerate(((w1, w1h), (w3, w3h))):
                dve.wait_ge(S("high_ready"), n + 1)
                dve.tensor_tensor(w[:].bitcast(F32R), w[:], high, ALU.subtract).then_inc(S("split_ready"), 1)

            def take_x(j, b, first=False):
                dve.wait_ge(S("tile_turned"), j + 1)
                if not first:
                    dve.wait_ge(S("up_ready"), j - 1)
                dve.tensor_copy(xTh[b % 2][:].bitcast(F32R), pXt[:, 0:P]).then_inc(S("xh_ready"), 1)
                dve.wait_ge(S("xh_ready"), j + 1)
                dve.tensor_tensor(xTl[b % 2][:].bitcast(F32R), pXt[:, 0:P], xTh[b % 2][:], ALU.subtract).then_inc(S("xT_ready"), 1)

            def hidden(j, b, first=False):
                dve.wait_ge(S("silu_ready"), j + 1)
                dve.wait_ge(S("up_ready"), j + 1)
                if not first:
                    dve.wait_ge(S("h_turned"), j - 1)
                dve.tensor_tensor(hh[b % 2][:], sg[b % 2][:], pUp[b % 2][:], ALU.mult).then_inc(S("h_ready"), 1)

            def take_h(j, b, first=False):
                dve.wait_ge(S("h_turned"), j + 1)
                if not first:
                    dve.wait_ge(S("down_ready"), j - 1)
                dve.tensor_copy(hhT[b % 2][:], pHt[b % 2][:]).then_inc(S("hT_done"), 1)

            def tile_step(s, b):
                flat = isinstance(s, int)
                if not flat or s + 1 < NT:
                    take_x(s + 1, (b + 1) % RING, first=flat and s < 1)
                if not flat or s < NT:
                    hidden(s, b, first=flat and s < 2)
                if not flat or s >= 1:
                    take_h(s - 1, (b - 1) % RING, first=flat and s < 3)

            take_x(0, 0, first=True)
            for s in range(RING):
                tile_step(s, s)
            with dve.Fori(0, NT // RING - 2, 1) as i:
                for b in range(RING):
                    tile_step(i * RING + (RING + b), b)
            for s in range(NT - RING, NT + 1):
                tile_step(s, s % RING)

            for c in range(NCH):
                ks = slice(c * TILES, (c + 1) * TILES)
                y0, y1 = (y[:, ks, :] for y in ych)
                dve.wait_ge(S(f"y_loaded{c}"), 32)
                dve.tensor_tensor(y0, y0, y1, ALU.add).then_inc(S("ysum"), 1)
                dve.wait_ge(S("ysum"), c + 1)
                gb = bc(gates[:, c * SEQS:(c + 1) * SEQS, 1, :], 2, TILES // SEQS)
                y0s = y0.rearrange("p (s k) c -> p s k c", s=SEQS)
                dve.tensor_tensor(y0s, y0s, gb, ALU.mult).then_inc(S("ygated"), 1)
                dve.wait_ge(S("ygated"), c + 1)
                dve.tensor_tensor(xs[:, ks, :], xs[:, ks, :], y0, ALU.add).then_inc(S("out_ready"), 1)


def kernel(L0_attn_x, L0_attn_time_decay, L0_attn_time_first, L0_attn_time_mix_k, L0_attn_time_mix_v,
           L0_attn_time_mix_r, L0_attn_Wk, L0_attn_Wv, L0_attn_Wr, L0_attn_Wo, L0_ffn_gate_w, L0_ffn_w1,
           L0_ffn_w2, L0_ffn_w3, L0_c, L0_wmod):
    import numpy as np
    import concourse.bacc as bacc
    from concourse.bass_utils import run_bass_kernel_spmd

    a = np.asarray
    arrays = {
        "x": a(L0_attn_x),
        "par": np.stack([a(v).reshape(-1) for v in (L0_attn_time_decay, L0_attn_time_first, L0_attn_time_mix_k,
                                                    L0_attn_time_mix_v, L0_attn_time_mix_r)], 1),
        "wproj": np.stack([a(w).T for w in (L0_attn_Wk, L0_attn_Wv, L0_attn_Wr, L0_attn_Wo)], 1),
        "gatew": a(L0_ffn_gate_w).T,
        "w1": a(L0_ffn_w1).transpose(2, 0, 1).reshape(P, E * F),
        "w3": a(L0_ffn_w3).transpose(2, 0, 1).reshape(P, E * F),
        "w2": a(L0_ffn_w2).reshape(E, C, FB, P).transpose(3, 0, 2, 1).reshape(P, E * F),
        "cT": a(L0_c).T,
        "wmod": a(L0_wmod),
    }
    arrays = {k: np.ascontiguousarray(v) for k, v in arrays.items()}
    nc = bacc.Bacc("TRN2", target_bir_lowering=False, num_devices=1)
    aps = [nc.dram_tensor("in_" + k, v.shape, mybir.dt.from_np(v.dtype), kind="ExternalInput").ap()
           for k, v in arrays.items()]
    out = nc.dram_tensor("out", (B, T, C), F32, kind="ExternalOutput").ap()
    block_program(nc, *aps, out)
    r = run_bass_kernel_spmd(nc, [{"in_" + k: v for k, v in arrays.items()}], core_ids=[0])
    return r.results[0]["out"]
```

```python
from contextlib import ExitStack

import concourse.bass as bass
from concourse import mybir

F32 = mybir.dt.float32
F32R = mybir.dt.float32r
BF16 = mybir.dt.bfloat16
I32 = mybir.dt.int32
U32 = mybir.dt.uint32
ALU = mybir.AluOpType
ACT = mybir.ActivationFunctionType
AX_X = mybir.AxisListType.X

P = 128
B, T, C = 16, 256, 128
TOKENS = B * T
E, F = 8, 512
FB = F // P
CHUNK = 512
SEQS = CHUNK // T
TILES = CHUNK // P
NCH = TOKENS // CHUNK
PAIRT = 2 * TILES
REGION = TOKENS + P
DUMMY = E * REGION
ROW = C + 2
NT = (2 * TOKENS + E * (P - 1)) // P
RING = 8
ROUNDED = NT // RING * RING
PAIR_DMAS = 16 * 2 * PAIRT
NEG = -1e38
DROP = -3e38
NOWHERE = 1 << 20
EPS = 1e-5
JITTER2 = 0.02


def bc(ap, axis, n):
    u = ap.unsqueeze(axis)
    shape = list(u.shape)
    shape[axis] = n
    return u.to_broadcast(shape)


def block_program(nc, x_d, par_d, wproj_d, gatew_d, w1_d, w3_d, w2_d, cT_d, wmod_d, out_d):
    with ExitStack() as ctx:
        def sb(name, shape, dt=F32):
            return ctx.enter_context(nc.sbuf_tensor(name, shape, dt))

        sems = {}

        def S(name):
            if name not in sems:
                sems[name] = ctx.enter_context(nc.semaphore(name))
            return sems[name]

        rows_d = nc.dram_tensor("expert_rows", [DUMMY + P, ROW], F32, kind="Internal").ap()
        y_d = nc.dram_tensor("choice_rows", [2 * TOKENS, C], F32, kind="Internal").ap()
        gates_d = nc.dram_tensor("gate_scratch", [B, 2 * C], F32, kind="Internal").ap()

        bank = [ctx.enter_context(nc.psum_tensor(f"bank{i}", [P, 512], F32)) for i in range(8)]
        pK, pV, pR, pXn, pXn2, pBack, pAttn, pSmall = bank
        pGate, pUp, pHt, pXt, pY = bank[0:2], bank[2:4], bank[4:6], bank[6], bank[7]
        pLogit = pSmall[:, 0:TILES * E]
        pRank = pAttn[:, 0:PAIRT * E]
        pCount = pAttn[:, 128:128 + E]

        ident = sb("ident", [P, P])
        before = sb("before", [P, P], BF16)
        ones = sb("ones", [P, P], BF16)
        ones8 = sb("ones8", [P, E])
        eps = sb("eps", [P, 1])
        par = sb("par", [P, 5])
        wproj = sb("wproj", [P, 4, C])
        wnow = sb("wnow", [P, 3, C])
        wprev = sb("wprev", [P, 3, C])
        gatew = sb("gatew", [P, E])
        w1 = sb("w1", [P, E * F])
        w3 = sb("w3", [P, E * F])
        w2 = sb("w2", [P, E * F])
        cT = sb("cT", [P, B])
        cexp = sb("cexp", [P, B])
        cinv = sb("cinv", [P, B])
        csilu = sb("csilu", [P, B])
        wmod = sb("wmod", [P, 6 * C])
        mods = sb("mods", [P, 4, B])
        gsign = sb("gsign", [B, 2 * C])
        gabs = sb("gabs", [B, 2 * C])
        graw = sb("graw", [B, 2 * C])
        gone = sb("gone", [B, 2 * C])
        gfix = sb("gfix", [B, 2 * C])
        gates = sb("gates", [P, B, 2, C])
        wog = sb("wog", [P, B, C])
        edecay = sb("edecay", [P, 1])
        wdecay = sb("wdecay", [P, 1])
        first_neg = sb("first_neg", [P, 1])
        prio = sb("prio", [P, E])
        ereg = sb("ereg", [P, E])
        eoff = sb("eoff", [P, E])
        thr = sb("thr", [P, TOKENS // P])
        pcol = sb("pcol", [P, 2])
        ids = sb("ids", [P, 2, TOKENS // P], I32)
        padrow = sb("padrow", [P, ROW])

        arena = sb("arena", [P, 16 * CHUNK + 2])
        taken = [0]

        def carve(*shape):
            n = 1
            for d in shape:
                n *= d
            piece = arena[:, taken[0]:taken[0] + n]
            taken[0] += n
            if len(shape) == 3:
                return piece.rearrange("p (a b c) -> p a b c", a=shape[0], b=shape[1])
            if len(shape) == 2:
                return piece.rearrange("p (a b) -> p a b", a=shape[0])
            return piece

        w1h, w3h = arena[:, 0:E * F], arena[:, E * F:2 * E * F]

        xs = sb("xs", [P, TOKENS // P, C])
        bn1 = sb("bn1", [P, TILES, 6])
        mv1 = sb("mv1", [P, TILES, 2])
        lnv1 = sb("lnv1", [P, TILES])
        rstd1 = sb("rstd1", [P, TILES])
        shift1 = sb("shift1", [P, TILES])
        bn2 = sb("bn2", [P, TILES, 6])
        mv2 = sb("mv2", [P, TILES, 2])
        lnv2 = sb("lnv2", [P, TILES])
        rstd2 = sb("rstd2", [P, TILES])
        xn = sb("xn", [P, TILES, C])
        xn2 = sb("xn2", [P, TILES, C])
        hT = sb("hT", [P, 2, SEQS, T + 1])
        h2T = sb("h2T", [P, CHUNK])
        pmax = sb("pmax", [P, SEQS, T + 1])
        z = carve(CHUNK)
        fac = carve(2, 5, CHUNK)
        fv = carve(CHUNK)
        state = carve(2, CHUNK + 1)
        mean = carve(2, CHUNK)
        rabs = sb("rabs", [P, CHUNK])
        rexp = sb("rexp", [P, CHUNK])
        lden = sb("lden", [P, CHUNK])
        garg = sb("garg", [P, CHUNK])
        gfac = sb("gfac", [P, CHUNK])
        yT = sb("yT", [P, CHUNK])
        hrow = sb("hrow", [P, 2, 2, 2, TILES, ROW])

        LL = sb("LL", [P, 2, PAIRT, E])
        top = sb("top", [P, 2, PAIRT])
        eq = sb("eq", [P, 2, PAIRT, E])
        pick = sb("pick", [P, 2, PAIRT, E])
        pbest = sb("pbest", [P, 2, PAIRT])
        hot = sb("hot", [P, 2, PAIRT, E])
        hots = sb("hots", [P, PAIRT, E], BF16)
        dif = sb("dif", [P, 2, PAIRT, E])
        mag = sb("mag", [P, 2, PAIRT, E])
        lim = sb("lim", [P, 2, PAIRT, E])
        keep = sb("keep", [P, 2, PAIRT, E])
        dexp = sb("dexp", [P, 2, PAIRT, E])
        kexp = sb("kexp", [P, 2, PAIRT, E])
        ksum = sb("ksum", [P, 2, PAIRT])
        base = sb("base", [P, E])
        pos = sb("pos", [P, PAIRT, E])
        hpos = sb("hpos", [P, 2, PAIRT, E])
        slot = sb("slot", [P, 2, PAIRT], I32)
        slot_last = sb("slot_last", [P, 2, 2, PAIRT], I32)
        ends_row = sb("ends_row", [1, E], I32)

        cnt = sb("cnt", [P, E])
        more = sb("more", [P, E, TOKENS // P])
        ntile = sb("ntile", [P, E])
        tend = sb("tend", [P, E])
        tstart = sb("tstart", [P, E])
        started = sb("started", [P, E])
        ended = sb("ended", [P, E])
        inside = sb("inside", [P, E])
        rbase = sb("rbase", [P, E])
        rowv = sb("rowv", [P, E])
        prod = sb("prod", [P, 2, E])
        sums = sb("sums", [P, 2])
        plan = sb("plan", [P, 2])
        table = sb("table", [1, 2, NT], I32)

        X = [sb(f"X{i}", [P, ROW]) for i in range(RING)]
        xTh = [sb(f"xTh{i}", [P, P]) for i in range(2)]
        xTl = [sb(f"xTl{i}", [P, P]) for i in range(2)]
        sg = [sb(f"sg{i}", [P, F]) for i in range(2)]
        hh = [sb(f"hh{i}", [P, F]) for i in range(2)]
        hhT = [sb(f"hhT{i}", [P, F]) for i in range(2)]
        yy = [sb(f"yy{i}", [P, C]) for i in range(RING)]
        ych = [w[:].rearrange("p (k c) -> p k c", c=C) for w in (w1, w3)]

        seq2 = lambda ap: ap.rearrange("p (s t) -> p s t", s=SEQS)
        til = lambda ap: ap.rearrange("p (k c) -> p k c", k=TILES)

        def settle(eng):
            eng.sem_inc(S(f"settled_{eng.engine.name}"), 1)

        block = ctx.enter_context(nc.Block())

        def front(step):
            step.loop = 0
            for c in range(2):
                step(c)
            with step.engine.Fori(0, (NCH - 4) // 2, 1) as i:
                step.loop = i
                step(i * 2 + 2)
                step(i * 2 + 3, odd=True)
            for c in range(NCH - 2, NCH + 1):
                step(c, odd=c == NCH - 1)

        def step_kind(c):
            flat = isinstance(c, int)
            return flat and c == 0, not flat or c < NCH - 1, not flat or c < NCH - 2, not flat or c < NCH

        SINGLE = NCH // 2 - 2
        ROUNDS = SINGLE + 4

        def window(r):
            if isinstance(r, int) and r >= SINGLE:
                half = (r - SINGLE) % 2
                return slice(half * TILES, (half + 1) * TILES)
            return slice(0, PAIRT)

        def pair_of(r):
            return r if r < SINGLE else SINGLE + (r - SINGLE) // 2

        def par_of(c, odd):
            return c % 2 if isinstance(c, int) else int(odd)

        def round_of(c, loop, odd):
            if isinstance(c, int):
                return None if c < 3 else c - (NCH - 2) + SINGLE
            return loop if odd else None

        @block.sync
        def _(sp):
            xv = x_d.rearrange("b (h p) c -> p (b h) c", p=P)
            first, second = slice(0, TILES), slice(TILES, 2 * TILES)
            sp.dma_start(xs[:, first, :], xv[:, first, :]).then_inc(S("x_first"), 16)
            sp.dma_start(cT[:], cT_d).then_inc(S("cond_loaded"), 16)
            sp.dma_start(par[:], par_d).then_inc(S("par_loaded"), 16)
            sp.dma_start(wproj[:], wproj_d).then_inc(S("wproj_loaded"), 16)
            sp.dma_start(wmod[:], wmod_d).then_inc(S("wmod_loaded"), 16)
            sp.dma_start(xs[:, second, :], xv[:, second, :]).then_inc(S("x_second"), 16)
            sp.dma_start(xs[:, 2 * TILES:, :], xv[:, 2 * TILES:, :]).then_inc(S("x_rest"), 16)
            sp.dma_start(gatew[:], gatew_d).then_inc(S("gatew_loaded"), 16)
            sp.wait_ge(S("gfix_ready"), 1)
            sp.dma_start(gates_d, gfix[:]).then_inc(S("gates_stored"), 16)
            sp.wait_ge(S("gates_stored"), 16)
            sp.dma_start(gates[:].rearrange("p b g c -> p (b g c)"),
                         gates_d.rearrange("b g -> (b g)").partition_broadcast(P)).then_inc(S("gates_loaded"), 16)
            sp.wait_ge(S("padrow_ready"), 2)
            sp.dma_start(rows_d[DUMMY:DUMMY + P, :], padrow[:]).then_inc(S("dummy_stored"), 16)
            sp.dma_start(w1[:], w1_d).then_inc(S("experts_loaded"), 16)
            sp.dma_start(w3[:], w3_d).then_inc(S("experts_loaded"), 16)
            sp.dma_start(w2[:], w2_d).then_inc(S("experts_loaded"), 16)

            sp.wait_ge(S("ends_ready"), 1)
            for e in range(E):
                row = sp.value_load(ends_row[0:1, e:e + 1], min_val=e * REGION, max_val=e * REGION + TOKENS)
                sp.dma_start(rows_d[bass.ds(row, P), :], padrow[:]).then_inc(S("pads_landed"), 16)

            def tile_row(j):
                return sp.value_load(table[0:1, 0, bass.ds(j, 1)], min_val=0, max_val=DUMMY)

            def load_tile(row, b):
                sp.dma_start(X[b][:], rows_d[bass.ds(row, P), :]).then_inc(S(f"tile_loaded{b}"), 16)

            sp.wait_ge(S("table_ready"), 1)
            ahead = [tile_row(b) for b in range(4)]
            sp.wait_ge(S("dummy_stored"), 16)
            sp.wait_ge(S("pads_landed"), 16 * E)
            sp.wait_ge(S("rows_landed"), PAIR_DMAS * NCH // 2)
            for b in range(RING):
                load_tile(ahead[b] if b < len(ahead) else tile_row(b), b)
            with sp.Fori(1, NT // RING, 1) as i:
                for b in range(RING):
                    sp.wait_ge(S(f"y_landed{b}"), i * 16)
                    load_tile(tile_row(i * RING + b), b)
            for b in range(NT - ROUNDED):
                sp.wait_ge(S(f"y_landed{b}"), 16 * ROUNDED // RING)
                load_tile(tile_row(ROUNDED + b), b)

            for b in range(RING):
                sp.wait_ge(S(f"y_landed{b}"), 16 * len(range(b, NT, RING)))
            yv = y_d.rearrange("(g k p) c -> p g k c", g=2, p=P)
            for c in range(NCH):
                for g in range(2):
                    sp.dma_start(ych[g][:, c * TILES:(c + 1) * TILES, :],
                                 yv[:, g, c * TILES:(c + 1) * TILES, :]).then_inc(S(f"y_loaded{c}"), 16)
            ov = out_d.rearrange("b (h p) c -> p (b h) c", p=P)
            for c in range(NCH):
                sp.wait_ge(S("out_ready"), c + 1)
                sp.dma_start(ov[:, c * TILES:(c + 1) * TILES, :],
                             xs[:, c * TILES:(c + 1) * TILES, :]).then_inc(S("out_stored"), 16)
            sp.wait_ge(S("out_stored"), 16 * NCH)

        @block.gpsimd
        def _(pool):
            pool.memset(ident[:], 0.0).then_inc(S("blank"), 1)
            pool.memset(before[:], 1.0).then_inc(S("blank"), 1)
            pool.memset(ones[:], 1.0).then_inc(S("ones_ready"), 1)
            pool.wait_ge(S("blank"), 2)
            pool.affine_select(out=ident[:], in_=ident[:], compare_op=ALU.not_equal, fill=1.0, base=0,
                               pattern=[[-1, P]], channel_multiplier=1).then_inc(S("ident_ready"), 1)
            pool.affine_select(out=before[:], in_=before[:], compare_op=ALU.is_gt, fill=0.0, base=0,
                               pattern=[[1, P]], channel_multiplier=-1).then_inc(S("before_ready"), 1)
            fl = dict(allow_small_or_imprecise_dtypes=True)
            pool.iota(prio[:], [[-1, E]], base=E, channel_multiplier=0, **fl).then_inc(S("tables"), 1)
            pool.iota(ereg[:], [[REGION, E]], base=0, channel_multiplier=0, **fl).then_inc(S("tables"), 1)
            pool.iota(eoff[:], [[F, E]], base=0, channel_multiplier=0, **fl).then_inc(S("tables"), 1)
            pool.iota(base[:], [[REGION, E]], base=0, channel_multiplier=0, **fl).then_inc(S("tables"), 1)
            pool.iota(thr[:], [[P, TOKENS // P]], base=0, channel_multiplier=0, **fl).then_inc(S("tables"), 1)
            pool.iota(pcol[:, 0:1], [[0, 1]], base=0, channel_multiplier=1, **fl).then_inc(S("tables"), 1)
            pool.iota(pcol[:, 1:2], [[0, 1]], base=0, channel_multiplier=P, **fl).then_inc(S("tables"), 1)
            pool.iota(ids[:], [[TOKENS, 2], [P, TOKENS // P]], base=0, channel_multiplier=1).then_inc(S("ids_ready"), 1)
            pool.memset(padrow[:], 0.0).then_inc(S("padrow_ready"), 1)
            pool.wait_ge(S("padrow_ready"), 1)
            pool.iota(padrow[:, C:C + 1].bitcast(I32), [[0, 1]], base=NOWHERE, channel_multiplier=0)\
                .then_inc(S("padrow_ready"), 1)
            pool.wait_ge(S("gates_loaded"), 16)
            pool.wait_ge(S("wproj_loaded"), 16)
            pool.tensor_tensor(wog[:], bc(wproj[:, 3, :], 1, B), gates[:, :, 0, :], ALU.mult)\
                .then_inc(S("wog_ready"), 1)
            pool.wait_ge(S("ids_ready"), 1)

            def address(q):
                for h in range(2):
                    m = pool.tensor_copy(hrow[:, q % 2, h, :, :, C].bitcast(I32),
                                         ids[:, :, q * PAIRT + h * TILES:q * PAIRT + (h + 1) * TILES])
                m.then_inc(S("dest_ready"), 1)

            address(0)
            address(1)
            pool.wait_ge(S("dest_ready"), 2)
            for r in range(ROUNDS):
                pool.wait_ge(S("slots_ready"), r + 1)
                pool.wait_ge(S("weights_ready"), r + 1)
                pool.wait_ge(S("rows_ready"), r * 2 + 2 if r < SINGLE else SINGLE + r + 1)
                q = pair_of(r)
                places = slot_last[:, q - SINGLE] if r >= SINGLE else slot
                w = window(r)
                for t in range(w.start, w.stop):
                    for g in range(2):
                        pool.indirect_dma_start(
                            rows_d, bass.IndirectOffsetOnAxis(ap=places[:, g, t:t + 1].bitcast(U32), axis=0),
                            hrow[:, q % 2, t // TILES, g, t % TILES, :], None).then_inc(S("rows_landed"), 16)
                if r < SINGLE:
                    pool.wait_ge(S("rows_landed"), PAIR_DMAS * (q + 1))
                    address(q + 2)
            def send(j, b):
                pool.wait_ge(S("y_ready"), j + 1)
                settle(pool)
                pool.indirect_dma_start(
                    y_d, bass.IndirectOffsetOnAxis(ap=X[b][:, C:C + 1].bitcast(U32), axis=0), yy[b][:], None,
                    bounds_check=2 * TOKENS - 1, oob_is_err=False).then_inc(S(f"y_landed{b}"), 16)

            with pool.Fori(0, NT // RING, 1) as i:
                for b in range(RING):
                    send(i * RING + b, b)
            for j in range(ROUNDED, NT):
                send(j, j % RING)

        @block.tensor
        def _(pe):
            pe.wait_ge(S("wmod_loaded"), 16)
            pe.wait_ge(S("csilu_ready"), 1)
            for n, j in enumerate((0, 1, 3, 4)):
                pe.matmul(pAttn[:, n * B:(n + 1) * B], wmod[:, j * C:(j + 1) * C], csilu[:], start=True, stop=True)
            for n, j in enumerate((2, 5)):
                m = pe.matmul(pBack[0:B, n * C:(n + 1) * C], csilu[:], wmod[:, j * C:(j + 1) * C],
                              start=True, stop=True)
            m.then_inc(S("mods_ready"), 1)
            pe.wait_ge(S("ident_ready"), 1)

            def turn1(c, first=False):
                pe.wait_ge(S("xn_ready"), c + 1)
                if not first:
                    pe.wait_ge(S("hT_ready"), c)
                for k in range(TILES):
                    m = pe.transpose(pXn[:, k * P:(k + 1) * P], xn[:, k, :], ident[:])
                m.then_inc(S("xnT_ready"), 1)

            def project(n, buf, dst, done):
                pe.matmul(seq2(dst[:]), wnow[:, n, :], hT[:, buf, :, 1:], start=True, stop=False)
                pe.matmul(seq2(dst[:]), wprev[:, n, :], hT[:, buf, :, 0:T], start=False, stop=True).then_inc(S(done), 1)

            def proj_k(c, buf, first=False):
                pe.wait_ge(S("hT_ready"), c + 1)
                if not first:
                    pe.wait_ge(S("z_ready"), c)
                project(0, buf, pK, "k_ready")

            def proj_v(c, buf, first=False):
                if not first:
                    pe.wait_ge(S("vprods_ready"), c)
                project(1, buf, pV, "v_ready")

            def proj_r(c, buf, first=False):
                if not first:
                    pe.wait_ge(S("garg_ready"), c)
                project(2, buf, pR, "r_ready")

            def ranks(r):
                pe.wait_ge(S("hots_ready"), r + 1)
                pe.wait_ge(S("x1_ready"), ranks.step)
                w = window(r)
                n = w.stop - w.start
                hv = hots[:, w, :].rearrange("p t e -> p (t e)")
                pe.matmul(pRank[:, 0:n * E], before[:], hv, start=True, stop=False)
                for d in range(1, n):
                    m = pe.matmul(pRank[:, d * E:n * E], ones[:], hv[:, 0:(n - d) * E], start=False, stop=d == n - 1)
                for t in range(n):
                    m = pe.matmul(pCount, ones[:], hv[:, t * E:(t + 1) * E], start=t == 0, stop=t == n - 1)
                m.then_inc(S("ranks_ready"), 1)

            def step(c, odd=False):
                is0, has1, has2, has = step_kind(c)
                nxt = 1 - par_of(c, odd)
                if has1:
                    proj_k(c + 1, nxt)
                r = round_of(c, step.loop, odd)
                ranks.step = c
                if r is not None and not has:
                    ranks(r)
                if not is0:
                    pe.wait_ge(S("xn2_ready"), c)
                    for k in range(TILES):
                        m = pe.transpose(pXn2[:, k * P:(k + 1) * P], xn2[:, k, :], ident[:])
                    m.then_inc(S("xn2T_ready"), 1)
                if r is not None and has:
                    ranks(r)
                if has1:
                    proj_v(c + 1, nxt)
                if not is0:
                    pe.wait_ge(S("h2T_ready"), c)
                    for k in range(TILES):
                        m = pe.matmul(pLogit[:, k * E:(k + 1) * E], h2T[:, k * P:(k + 1) * P], gatew[:],
                                      start=True, stop=True)
                    m.then_inc(S("logits_ready"), 1)
                    if not (isinstance(c, int) and c == 1):
                        pe.wait_ge(S("rows_ready"), c - 1)
                    for k in range(TILES):
                        m = pe.transpose(pBack[:, k * P:(k + 1) * P], h2T[:, k * P:(k + 1) * P], ident[:])
                    m.then_inc(S("back_ready"), 1)
                if has2:
                    turn1(c + 2)
                if has:
                    if is0:
                        pe.wait_ge(S("wog_ready"), 1)
                    else:
                        pe.wait_ge(S("x1_ready"), c)
                    if r is not None:
                        pe.wait_ge(S("ranks_read"), r + 1)
                    pe.matmul(pAttn[:], ident[:], xs[:, bass.ds(c * TILES, TILES), :], start=True, stop=False)
                    pe.wait_ge(S("yT_ready"), c + 1)
                    for k in range(TILES):
                        m = pe.matmul(pAttn[:, k * P:(k + 1) * P], yT[:, k * P:(k + 1) * P],
                                      wog[:, bass.ds(c * SEQS + k // (TILES // SEQS), 1), :],
                                      start=False, stop=k == TILES - 1)
                    m.then_inc(S("attn_ready"), 1)
                if has1:
                    proj_r(c + 1, nxt)

            step.engine = pe
            turn1(0, first=True)
            pe.wait_ge(S("proj_ready"), 1)
            proj_k(0, 0, first=True)
            proj_v(0, 0, first=True)
            turn1(1)
            proj_r(0, 0, first=True)
            pe.wait_ge(S("gatew_loaded"), 16)
            pe.wait_ge(S("before_ready"), 1)
            pe.wait_ge(S("ones_ready"), 1)
            front(step)

            ranks(ROUNDS - 1)

            pe.wait_ge(S("plan_ready"), 1)
            for n in range(2):
                m = pe.transpose(pSmall[0:1, 256 + n * NT:256 + (n + 1) * NT], plan[0:NT, n:n + 1], ident[0:NT, 0:NT])
            m.then_inc(S("planT_ready"), 1)

            pe.wait_ge(S("table_ready"), 1)
            pe.wait_ge(S("experts_loaded"), 48)
            pe.wait_ge(S("split_ready"), 2)

            def turn_x(j, b, u, first=False, dst=pXt):
                pe.wait_ge(S(f"tile_loaded{b}"), u)
                if not first:
                    pe.wait_ge(S("xT_ready"), j)
                pe.transpose(dst[:, 0:P], X[b][:, 0:C], ident[:]).then_inc(S("tile_turned"), 1)

            def weights_of(j):
                return pe.value_load(table[0:1, 1, bass.ds(j, 1)], min_val=0, max_val=(E - 1) * F)

            def gate_up(j, b, off, first=False):
                pe.wait_ge(S("xT_ready"), j + 1)
                if not first:
                    pe.wait_ge(S("h_ready"), j - 1)
                xh, xl = xTh[b % 2][:].bitcast(F32R), xTl[b % 2][:].bitcast(F32R)
                for dst, high, low, done in ((pGate, w1h, w1, "gate_ready"), (pUp, w3h, w3, "up_ready")):
                    wh, wl = (t[:, bass.ds(off, F)].bitcast(F32R) for t in (high, low))
                    pe.matmul(dst[b % 2][:], xh, wh, start=True, stop=False)
                    pe.matmul(dst[b % 2][:], xh, wl, start=False, stop=False)
                    pe.matmul(dst[b % 2][:], xl, wh, start=False, stop=True).then_inc(S(done), 1)

            def turn_h(j, b, first=False):
                pe.wait_ge(S("h_ready"), j + 1)
                if not first:
                    pe.wait_ge(S("hT_done"), j - 1)
                for k in range(FB):
                    m = pe.transpose(pHt[b % 2][:, k * P:(k + 1) * P], hh[b % 2][:, k * P:(k + 1) * P], ident[:])
                m.then_inc(S("h_turned"), 1)

            def down(j, b, off, first=False):
                pe.wait_ge(S("hT_done"), j + 1)
                if not first:
                    pe.wait_ge(S("y_ready"), j)
                for k in range(FB):
                    m = pe.matmul(pY[:, 0:C], hhT[b % 2][:, k * P:(k + 1) * P], w2[:, bass.ds(off + k * P, P)],
                                  start=k == 0, stop=k == FB - 1)
                m.then_inc(S("down_ready"), 1)

            def loads(j):
                return 16 * (j // RING + 1)

            def tile_step(s, b, offs, i=None):
                flat = isinstance(s, int)
                if not flat or s < NT:
                    gate_up(s, b, offs[b], first=flat and s < 2)
                if not flat or s + 1 < NT:
                    offs[b + 1] = weights_of(s + 1)
                if not flat or 0 < s < NT - 1:
                    turn_x(s + 1, (b + 1) % RING, loads(s + 1) if flat else i * 16 + 32 + 16 * ((b + 1) // RING))
                if not flat or 0 <= s - 1 < NT:
                    turn_h(s - 1, (b - 1) % RING, first=flat and s < 3)
                if not flat or s >= 2:
                    down(s - 2, (b - 2) % RING, offs[b - 2], first=flat and s < 3)

            over = {n: pe.alloc_register(f"weights_{name}")
                    for n, name in ((-2, "before_last"), (-1, "last"), (0, "next"))}

            def ring_start():
                return {n: pe.snap(over[n], min_val=0, max_val=(E - 1) * F) for n in over}

            def ring_end(offs):
                for n in over:
                    pe.reg_mov(over[n], offs[RING + n])

            turn_x(0, 0, loads(0), first=True)
            turn_x(1, 1, loads(1), first=True, dst=pY)
            offs = {0: weights_of(0)}
            for s in range(RING):
                tile_step(s, s, offs)
            ring_end(offs)
            with pe.Fori(0, NT // RING - 1, 1) as i:
                offs = ring_start()
                for b in range(RING):
                    tile_step(i * RING + (RING + b), b, offs, i)
                ring_end(offs)
            offs = ring_start()
            for b in range(NT - ROUNDED + 2):
                tile_step(ROUNDED + b, b, offs)

        @block.scalar
        def _(act):
            act.preload_act_table_set("natural_log_exp_and_others")
            act.wait_ge(S("cond_loaded"), 16)
            act.activation(cexp[:], cT[:], ACT.Exp, scale=-1.0).then_inc(S("cexp_ready"), 1)
            act.wait_ge(S("par_loaded"), 16)
            act.activation(edecay[:], par[:, 0:1], ACT.Exp).then_inc(S("edecay_ready"), 1)
            act.wait_ge(S("eps_ready"), 1)

            def inv_std(c, mv, lnv, rstd, moments, logged, ready):
                act.wait_ge(S(moments), c + 1)
                act.activation(lnv[:], mv[:, :, 1], ACT.Ln, bias=eps[:, 0:1]).then_inc(S(logged), 1)
                act.wait_ge(S(logged), c + 1)
                act.activation(rstd[:], lnv[:], ACT.Exp, scale=-0.5).then_inc(S(ready), 1)

            def std1(c):
                inv_std(c, mv1, lnv1, rstd1, "moments1_ready", "lnv1_ready", "rstd1_ready")

            def std2(c):
                inv_std(c, mv2, lnv2, rstd2, "moments2_ready", "lnv2_ready", "rstd2_ready")

            def norm(c, dst, rstd, shift, ready):
                for k in range(TILES):
                    m = act.activation(dst[:, k, :], xs[:, bass.ds(c * TILES + k, 1), :], ACT.Identity,
                                       scale=rstd[:, k:k + 1], bias=shift[:, k:k + 1])
                m.then_inc(S(ready), 1)

            def norm1(c):
                act.wait_ge(S("shift1_ready"), c + 1)
                norm(c, xn, rstd1, shift1, "xn_ready")

            def factors(c, buf, n):
                act.wait_ge(S("z_ready"), c + 1)
                plus, minus = ((edecay[:, 0:1], wdecay[:, 0:1]), (par[:, 1:2], first_neg[:, 0:1]))[n]
                pair = fac[:, buf, 2 * n:2 * n + 2, :]
                act.activation(pair[:, 0, :], z[:], ACT.Relu, bias=plus)
                act.activation(pair[:, 1, :], z[:], ACT.Relu, scale=-1.0, bias=minus).then_inc(S("args_ready"), 1)
                act.wait_ge(S("args_ready"), c * 2 + (n + 1))
                act.activation(pair, pair, ACT.Exp, scale=-1.0).then_inc(S("facs_ready"), 1)

            def modulate1(c, buf, first=False):
                act.wait_ge(S("xnT_ready"), c + 1)
                if not first:
                    act.wait_ge(S("r_ready"), c - 1)
                for s in range(SEQS):
                    m = act.activation(hT[:, buf, s, 1:], pXn[:, s * T:(s + 1) * T], ACT.Identity,
                                       scale=mods[:, 1, bass.ds(c * SEQS + s, 1)],
                                       bias=mods[:, 0, bass.ds(c * SEQS + s, 1)])
                m.then_inc(S("hT_ready"), 1)

            def modulate2(c):
                act.wait_ge(S("xn2T_ready"), c + 1)
                for s in range(SEQS):
                    m = act.activation(h2T[:, s * T:(s + 1) * T], pXn2[:, s * T:(s + 1) * T], ACT.Identity,
                                       scale=mods[:, 3, bass.ds(c * SEQS + s, 1)],
                                       bias=mods[:, 2, bass.ds(c * SEQS + s, 1)])
                m.then_inc(S("h2T_ready"), 1)

            def step(c, odd=False):
                is0, has1, has2, has = step_kind(c)
                buf = par_of(c, odd)
                if has2:
                    std1(c + 2)
                if not is0:
                    act.wait_ge(S("moments2_ready"), c)
                    act.activation(xs[:, bass.ds((c - 1) * TILES, TILES), :], til(pAttn[:]), ACT.Copy)\
                        .then_inc(S("x1_ready"), 1)
                    std2(c - 1)
                if has:
                    factors(c, buf, 1)
                if has2:
                    norm1(c + 2)
                if has:
                    act.wait_ge(S("r_ready"), c + 1)
                    act.activation(rabs[:], pR[:], ACT.Abs).then_inc(S("rabs_ready"), 1)
                    act.wait_ge(S("rabs_ready"), c + 1)
                    act.activation(rexp[:], rabs[:], ACT.Exp, scale=-1.0).then_inc(S("rexp_ready"), 1)
                r = round_of(c, step.loop, odd)
                if r is not None and not has:
                    likely(r)
                if not is0:
                    modulate2(c - 1)
                if r is not None and has:
                    likely(r)
                if has:
                    act.wait_ge(S("den_ready"), c + 1)
                    act.activation(lden[:], mean[:, 0, :], ACT.Ln).then_inc(S("lden_ready"), 1)
                    act.wait_ge(S("garg_ready"), c + 1)
                    act.activation(gfac[:], garg[:], ACT.Exp).then_inc(S("gfac_ready"), 1)
                if has1:
                    factors(c + 1, 1 - buf, 0)
                if has2:
                    modulate1(c + 2, buf)
                if not is0:
                    flat = isinstance(c, int)
                    pair = (c - 1) // 2 if flat else step.loop + int(odd)
                    half = (c - 1) % 2 if flat else int(not odd)
                    parity = pair % 2 if flat else step.loop * -1 + 1 if odd else step.loop
                    act.wait_ge(S("back_ready"), c)
                    act.wait_ge(S("dest_ready"), pair + 1)
                    act.activation(hrow[:, bass.ds(parity, 1), half, :, :, 0:C].squeeze(1),
                                   bc(til(pBack[:]), 1, 2), ACT.Copy).then_inc(S("rows_ready"), 1)

            def likely(r):
                act.wait_ge(S("dif_ready"), r + 1)
                w = window(r)
                act.activation(dexp[:, :, w, :], dif[:, :, w, :], ACT.Exp).then_inc(S("dexp_ready"), 1)

            step.engine = act
            std1(0)
            norm1(0)
            act.wait_ge(S("mods_fixed"), 1)
            modulate1(0, 0, first=True)
            std1(1)
            norm1(1)
            act.wait_ge(S("edges_ready"), 1)
            factors(0, 0, 0)
            modulate1(1, 1, first=True)
            front(step)
            likely(ROUNDS - 1)
            act.wait_ge(S("experts_loaded"), 48)
            for w, high in ((w1, w1h), (w3, w3h)):
                act.activation(high.bitcast(F32R), w[:], ACT.Copy).then_inc(S("high_ready"), 1)

            act.preload_act_table(ACT.Silu)

            def silu(j, b, first=False):
                act.wait_ge(S("gate_ready"), j + 1)
                if not first:
                    act.wait_ge(S("h_ready"), j - 1)
                act.activation(sg[b % 2][:], pGate[b % 2][:], ACT.Silu).then_inc(S("silu_ready"), 1)

            def weigh(j, b):
                act.wait_ge(S("down_ready"), j + 1)
                act.activation(yy[b][:], pY[:, 0:C], ACT.Copy, scale=X[b][:, C + 1:C + 2]).then_inc(S("y_ready"), 1)

            def tile_step(s, b):
                flat = isinstance(s, int)
                if not flat or s < NT:
                    silu(s, b, first=flat and s < 2)
                if not flat or s >= 2:
                    weigh(s - 2, (b - 2) % RING)

            for s in range(RING):
                tile_step(s, s)
            with act.Fori(0, NT // RING - 1, 1) as i:
                for b in range(RING):
                    tile_step(i * RING + (RING + b), b)
            for s in range(ROUNDED, NT + 2):
                tile_step(s, s % RING)

        @block.vector
        def _(dve):
            dve.memset(eps[:], EPS).then_inc(S("eps_ready"), 1)
            dve.memset(hT[:, :, :, 0], 0.0)
            dve.memset(pmax[:, :, 0], NEG)
            dve.memset(state[:, :, 0], 0.0)
            dve.memset(ones8[:], 1.0).then_inc(S("edges_ready"), 1)
            dve.wait_ge(S("cexp_ready"), 1)
            dve.tensor_scalar_add(cinv[:], cexp[:], 1.0).then_inc(S("cond"), 1)
            dve.wait_ge(S("cond"), 1)
            dve.reciprocal(cinv[:], cinv[:]).then_inc(S("cond"), 1)
            dve.wait_ge(S("cond"), 2)
            dve.tensor_tensor(csilu[:], cT[:], cinv[:], ALU.mult).then_inc(S("csilu_ready"), 1)

            def stats(c, rows, bn, mv, told, ready, go=None):
                for k in range(TILES):
                    m = dve.bn_stats(bn[:, k, :], rows(k))
                m.then_inc(S(told), 1)
                if go:
                    go()
                dve.wait_ge(S(told), c + 1)
                settle(dve)
                for k in range(TILES):
                    m = dve.bn_aggr(mv[:, k, :], bn[:, k, :])
                m.then_inc(S(ready), 1)

            def stats1(c):
                stats(c, lambda k: xs[:, bass.ds(c * TILES + k, 1), :], bn1, mv1, "stats1", "moments1_ready")

            def stats2(c, go):
                stats(c, lambda k: pAttn[:, k * P:(k + 1) * P], bn2, mv2, "stats2", "moments2_ready", go)

            def shift(c, sh, mv, rstd, known, ready):
                dve.wait_ge(S(known), c + 1)
                dve.scalar_tensor_tensor(sh[:], mv[:, :, 0], -1.0, rstd[:], ALU.mult, ALU.mult)\
                    .then_inc(S(ready), 1)

            def shift1_(c, first=False):
                if not first:
                    dve.wait_ge(S("xn_ready"), c)
                shift(c, shift1, mv1, rstd1, "rstd1_ready", "shift1_ready")

            def norm2(c, go):
                dve.wait_ge(S("rstd2_ready"), c + 1)
                for t in range(TILES):
                    m = dve.tensor_scalar(xn2[:, t, :], xs[:, bass.ds(c * TILES + t, 1), :], mv2[:, t, 0:1],
                                          rstd2[:, t:t + 1], ALU.subtract, ALU.mult)
                    if t == TILES // 2:
                        go()
                m.then_inc(S("xn2_ready"), 1)

            dve.wait_ge(S("x_first"), 16)
            stats1(0)
            dve.wait_ge(S("par_loaded"), 16)
            dve.wait_ge(S("wproj_loaded"), 16)
            for n in range(3):
                m = dve.tensor_scalar(wnow[:, n, :], wproj[:, n, :], par[:, 2 + n:3 + n], None, ALU.mult)
            m.then_inc(S("wnow_ready"), 1)
            shift1_(0, first=True)
            dve.wait_ge(S("wnow_ready"), 1)
            dve.tensor_tensor(wprev[:], wproj[:, 0:3, :], wnow[:], ALU.subtract).then_inc(S("proj_ready"), 1)
            dve.wait_ge(S("mods_ready"), 1)
            mp = pAttn[:, 0:4 * B].rearrange("p (m b) -> p m b", m=4)
            for m_, one in ((0, 0.0), (1, 1.0), (2, 0.0), (3, 1.0)):
                m = dve.tensor_scalar_add(mods[:, m_, :], mp[:, m_, :], one)
            m.then_inc(S("mods_fixed"), 1)
            gp = pBack[0:B, 0:2 * C]
            dve.tensor_scalar(gsign[:], gp, 0.0, 2.0, ALU.is_ge, ALU.mult).then_inc(S("gate_parts"), 1)
            dve.tensor_copy(graw[:], gp).then_inc(S("gate_parts"), 1)
            dve.wait_ge(S("gate_parts"), 2)
            dve.scalar_tensor_tensor(gabs[:], graw[:], -1.0, graw[:], ALU.mult, ALU.max).then_inc(S("gate_parts"), 1)
            dve.tensor_scalar_add(gone[:], gsign[:], -1.0).then_inc(S("gate_parts"), 1)
            dve.wait_ge(S("gate_parts"), 4)
            dve.scalar_tensor_tensor(gfix[:], gabs[:], 0.25, gone[:], ALU.max, ALU.mult).then_inc(S("gfix_ready"), 1)
            dve.wait_ge(S("edecay_ready"), 1)
            dve.tensor_scalar(first_neg[:], par[:, 1:2], -1.0, None, ALU.mult).then_inc(S("wdecay_ready"), 1)
            dve.tensor_scalar(wdecay[:], edecay[:], -1.0, None, ALU.mult).then_inc(S("wdecay_ready"), 1)
            dve.wait_ge(S("x_second"), 16)
            stats1(1)
            shift1_(1)
            dve.wait_ge(S("edges_ready"), 1)
            dve.wait_ge(S("wdecay_ready"), 2)
            dve.wait_ge(S("tables"), 7)

            def decay_args(c):
                dve.wait_ge(S("k_ready"), c + 1)
                for s in range(SEQS):
                    m = dve.tensor_tensor_scan(pmax[:, s, 1:], wdecay[:, 0:1].to_broadcast([P, T]),
                                               pK[:, s * T:(s + 1) * T], NEG, ALU.add, ALU.max)
                m.then_inc(S("pmax_ready"), 1)
                dve.wait_ge(S("pmax_ready"), c + 1)
                dve.tensor_tensor(seq2(z[:]), seq2(pK[:]), pmax[:, :, 0:T], ALU.subtract).then_inc(S("z_ready"), 1)

            def states(c, buf, go):
                f1, f2 = fac[:, buf, 0, :], fac[:, buf, 1, :]
                dve.wait_ge(S("facs_ready"), c * 2 + 1)
                dve.wait_ge(S("v_ready"), c + 1)
                dve.tensor_tensor(fv, f2, pV[:], ALU.mult).then_inc(S("fv_ready"), 1)
                go()
                dve.tensor_tensor_scan(state[:, 0, 1:], f1, f2, 0.0, ALU.mult, ALU.add)
                go()
                dve.wait_ge(S("fv_ready"), c + 1)
                dve.tensor_tensor_scan(state[:, 1, 1:], f1, fv, 0.0, ALU.mult, ALU.add)\
                    .then_inc(S("states_ready"), 1)
                go()

            def means(c, buf, go):
                e1, e2, ev = (fac[:, buf, n, :] for n in range(2, 5))
                dve.wait_ge(S("facs_ready"), c * 2 + 2)
                dve.tensor_tensor(ev, e2, pV[:], ALU.mult).then_inc(S("vprods_ready"), 1)
                go()
                dve.wait_ge(S("states_ready"), c + 1)
                dve.tensor_tensor(mean, bc(e1, 1, 2), state[:, :, 0:CHUNK], ALU.mult).then_inc(S("old_ready"), 1)
                go()
                dve.wait_ge(S("vprods_ready"), c + 1)
                dve.wait_ge(S("old_ready"), c + 1)
                dve.tensor_tensor(mean, mean, fac[:, buf, 3:5, :], ALU.add).then_inc(S("mean_ready"), 1)
                go()
                dve.wait_ge(S("mean_ready"), c + 1)
                dve.wait_ge(S("rexp_ready"), c + 1)
                dve.scalar_tensor_tensor(mean[:, 0, :], rexp[:], 1.0, mean[:, 0, :], ALU.add, ALU.mult)\
                    .then_inc(S("den_ready"), 1)
                go()

            ROUTE = 14

            def route(r, k):
                if r is None:
                    return
                w = window(r)
                n = w.stop - w.start
                if k:
                    dve.wait_ge(S("route_step"), r * ROUTE + k)
                g, part = (0, k + 1) if k < 5 else (1, k - 5)
                logit, best, pri, chosen = LL[:, g, w, :], top[:, g, w], pick[:, g, w, :], hot[:, g, w, :]
                logits, d, lm, kp, mg = (t[:, :, w, :] for t in (LL, dif, lim, keep, mag))
                topb = bc(top[:, :, w], 3, E)
                if part == 0:
                    m = dve.scalar_tensor_tensor(logit, hot[:, 0, w, :], DROP, LL[:, 0, w, :], ALU.mult, ALU.add)
                elif part == 1:
                    m = dve.tensor_reduce(best, logit, AX_X, ALU.max)
                elif part == 2:
                    m = dve.tensor_tensor(eq[:, g, w, :], logit, bc(best, 2, E), ALU.is_equal)
                elif part == 3:
                    m = dve.tensor_tensor(pri, eq[:, g, w, :], bc(prio[:], 1, n), ALU.mult)
                elif part == 4:
                    m = dve.tensor_reduce(pbest[:, g, w], pri, AX_X, ALU.max)
                elif part == 5:
                    m = dve.tensor_tensor(chosen, pri, bc(pbest[:, g, w], 2, E), ALU.is_equal)
                elif part == 6:
                    dve.tensor_tensor(hots[:, w, :], hot[:, 0, w, :], hot[:, 1, w, :], ALU.add)\
                        .then_inc(S("hots_ready"), 1)
                    dve.tensor_tensor(d, logits, topb, ALU.subtract).then_inc(S("dif_ready"), 1)
                    m = dve.scalar_tensor_tensor(mg, logits, -1.0, logits, ALU.mult, ALU.max)
                elif part == 7:
                    m = dve.tensor_tensor(lm, mg, topb, ALU.max)
                elif part == 8:
                    dve.wait_ge(S("dif_ready"), r + 1)
                    m = dve.scalar_tensor_tensor(kp, lm, -JITTER2, d, ALU.mult, ALU.is_le)
                m.then_inc(S("route_step"), 1)

            def router(r):
                done = [0]

                def go(n=1):
                    for k in range(done[0], min(done[0] + n, STAGES)):
                        route(r, k)
                    done[0] += n

                return go

            STAGES = 14

            def place(r):
                w = window(r)
                n = w.stop - w.start
                dve.wait_ge(S("ranks_ready"), r + 1)
                dve.tensor_tensor(pos[:, w, :], pRank[:, 0:n * E].rearrange("p (t e) -> p t e", e=E),
                                  bc(base[:], 1, n), ALU.add).then_inc(S("pos_ready"), 1)
                dve.wait_ge(S("pos_ready"), r + 1)
                dve.tensor_tensor(base[:], base[:], pCount, ALU.add).then_inc(S("ranks_read"), 1)
                dve.tensor_tensor(hpos[:, :, w, :], hot[:, :, w, :], bc(pos[:, w, :], 1, 2), ALU.mult)\
                    .then_inc(S("hpos_ready"), 1)

            def weigh(r):
                w = window(r)
                flat = isinstance(r, int)
                slots = slot_last[:, pair_of(r) - SINGLE] if flat else slot
                dve.wait_ge(S("route_step"), r * ROUTE + STAGES)
                dve.wait_ge(S("dexp_ready"), r + 1)
                dve.tensor_tensor(kexp[:, :, w, :], keep[:, :, w, :], dexp[:, :, w, :], ALU.mult)\
                    .then_inc(S("kexp_ready"), 1)
                dve.wait_ge(S("dest_ready"), pair_of(r) + 1 if flat else r + 2)
                dve.wait_ge(S("hpos_ready"), r + 1)
                with nc.allow_low_precision(reason="row numbers are whole and under 2**24"):
                    dve.tensor_reduce(slots[:, :, w], hpos[:, :, w, :], AX_X, ALU.add)\
                        .then_inc(S("slots_ready"), 1)
                dve.wait_ge(S("kexp_ready"), r + 1)
                dve.tensor_reduce(ksum[:, :, w], kexp[:, :, w, :], AX_X, ALU.add).then_inc(S("ksum_ready"), 1)
                dve.wait_ge(S("ksum_ready"), r + 1)
                dve.wait_ge(S("ranks_read"), r + 1)
                settle(dve)
                parity = pair_of(r) % 2 if flat else r
                for h in range(w.start // TILES, w.stop // TILES):
                    m = dve.reciprocal(hrow[:, bass.ds(parity, 1), h, :, :, C + 1].squeeze(1),
                                       ksum[:, :, h * TILES:(h + 1) * TILES])
                m.then_inc(S("weights_ready"), 1)

            def step(c, odd=False):
                is0, has1, has2, has = step_kind(c)
                r = round_of(c, step.loop, odd)
                if is0:
                    dve.wait_ge(S("x_rest"), 16)
                if has2:
                    stats1(c + 2)
                go = router(r)
                go(2 if has2 else 10)
                if not is0:
                    go()
                    dve.wait_ge(S("attn_ready"), c)
                    settle(dve)
                    stats2(c - 1, go)
                if has:
                    go()
                    states(c, par_of(c, odd), go)
                    if has2:
                        shift1_(c + 2)
                    go()
                    if not is0:
                        norm2(c - 1, go)
                    go()
                    means(c, par_of(c, odd), go)
                    go(STAGES)
                else:
                    norm2(c - 1, go)
                    go()
                    place(r)
                    weigh(r)
                if has1:
                    decay_args(c + 1)
                if r is not None and has:
                    place(r)
                if has:
                    dve.wait_ge(S("lden_ready"), c + 1)
                    dve.scalar_tensor_tensor(garg[:], pR[:], 0.0, lden[:], ALU.min, ALU.subtract)\
                        .then_inc(S("garg_ready"), 1)
                if r is not None and has:
                    weigh(r)
                if not is0:
                    half = (c - 1) % 2 if isinstance(c, int) else int(not odd)
                    dve.wait_ge(S("logits_ready"), c)
                    dve.tensor_copy(LL[:, 0, half * TILES:(half + 1) * TILES, :],
                                    pLogit.rearrange("p (t e) -> p t e", e=E)).then_inc(S("logits_read"), 1)
                if has:
                    dve.wait_ge(S("gfac_ready"), c + 1)
                    dve.tensor_tensor(yT[:], mean[:, 1, :], gfac[:], ALU.mult).then_inc(S("yT_ready"), 1)
                if not is0:
                    dve.wait_ge(S("logits_read"), c)

            step.engine = dve
            decay_args(0)
            front(step)
            router(ROUNDS - 1)(STAGES)
            place(ROUNDS - 1)
            weigh(ROUNDS - 1)

            made = [0]

            def link(m):
                made[0] += 1
                m.then_inc(S("plan_step"), 1)
                dve.wait_ge(S("plan_step"), made[0])

            dve.tensor_copy(ends_row[:], base[0:1, :]).then_inc(S("ends_ready"), 1)
            link(dve.tensor_tensor(cnt[:], base[:], ereg[:], ALU.subtract))
            link(dve.tensor_tensor(more[:], bc(cnt[:], 2, TOKENS // P), bc(thr[:], 1, E), ALU.is_gt))
            link(dve.tensor_reduce(ntile[:], more[:], AX_X, ALU.add))
            link(dve.tensor_tensor_scan(tend[:], ones8[:], ntile[:], 0.0, ALU.mult, ALU.add))
            link(dve.tensor_tensor(tstart[:], tend[:], ntile[:], ALU.subtract))
            link(dve.tensor_scalar(started[:], tstart[:], pcol[:, 0:1], None, ALU.is_le))
            link(dve.tensor_scalar(ended[:], tend[:], pcol[:, 0:1], None, ALU.is_le))
            link(dve.tensor_tensor(inside[:], started[:], ended[:], ALU.subtract))
            link(dve.scalar_tensor_tensor(rbase[:], tstart[:], -float(P), ereg[:], ALU.mult, ALU.add))
            link(dve.tensor_scalar(rowv[:], rbase[:], pcol[:, 1:2], None, ALU.add))
            link(dve.tensor_tensor(prod[:, 0, :], inside[:], rowv[:], ALU.mult))
            link(dve.tensor_tensor(prod[:, 1, :], inside[:], eoff[:], ALU.mult))
            link(dve.tensor_reduce(sums[:], prod[:], AX_X, ALU.add))
            dve.tensor_copy(plan[:, 1:2], sums[:, 1:2])
            dve.scalar_tensor_tensor(plan[:, 0:1], ended[:, E - 1:E], float(DUMMY), sums[:, 0:1],
                                     ALU.mult, ALU.add).then_inc(S("plan_ready"), 1)
            dve.wait_ge(S("planT_ready"), 1)
            dve.tensor_copy(table[:].rearrange("p n t -> p (n t)"), pSmall[0:1, 256:256 + 2 * NT])\
                .then_inc(S("table_ready"), 1)
            for n, (w, high) in enumerate(((w1, w1h), (w3, w3h))):
                dve.wait_ge(S("high_ready"), n + 1)
                dve.tensor_tensor(w[:].bitcast(F32R), w[:], high, ALU.subtract).then_inc(S("split_ready"), 1)

            def take_x(j, b, first=False, src=pXt):
                dve.wait_ge(S("tile_turned"), j + 1)
                if not first:
                    dve.wait_ge(S("up_ready"), j - 1)
                dve.tensor_copy(xTh[b % 2][:].bitcast(F32R), src[:, 0:P]).then_inc(S("xh_ready"), 1)
                dve.wait_ge(S("xh_ready"), j + 1)
                dve.tensor_tensor(xTl[b % 2][:].bitcast(F32R), src[:, 0:P], xTh[b % 2][:], ALU.subtract).then_inc(S("xT_ready"), 1)

            def hidden(j, b, first=False):
                dve.wait_ge(S("silu_ready"), j + 1)
                dve.wait_ge(S("up_ready"), j + 1)
                if not first:
                    dve.wait_ge(S("h_turned"), j - 1)
                dve.tensor_tensor(hh[b % 2][:], sg[b % 2][:], pUp[b % 2][:], ALU.mult).then_inc(S("h_ready"), 1)

            def take_h(j, b, first=False):
                dve.wait_ge(S("h_turned"), j + 1)
                if not first:
                    dve.wait_ge(S("down_ready"), j - 1)
                dve.tensor_copy(hhT[b % 2][:], pHt[b % 2][:]).then_inc(S("hT_done"), 1)

            def tile_step(s, b):
                flat = isinstance(s, int)
                if not flat or 0 < s < NT - 1:
                    take_x(s + 1, (b + 1) % RING)
                if not flat or s < NT:
                    hidden(s, b, first=flat and s < 2)
                if not flat or s >= 1:
                    take_h(s - 1, (b - 1) % RING, first=flat and s < 3)

            take_x(0, 0, first=True)
            take_x(1, 1, first=True, src=pY)
            for s in range(RING):
                tile_step(s, s)
            with dve.Fori(0, NT // RING - 1, 1) as i:
                for b in range(RING):
                    tile_step(i * RING + (RING + b), b)
            for s in range(ROUNDED, NT + 1):
                tile_step(s, s % RING)

            def chunk_of(t, c):
                return t[:, c * TILES:(c + 1) * TILES, :]

            for n in range(-1, NCH + 1):
                if 0 <= n < NCH:
                    y0 = chunk_of(ych[0], n)
                    dve.wait_ge(S("ysum"), n + 1)
                    gb = bc(gates[:, n * SEQS:(n + 1) * SEQS, 1, :], 2, TILES // SEQS)
                    split = lambda t: t.rearrange("p (s k) c -> p s k c", s=SEQS)
                    dve.tensor_tensor(split(y0), split(y0), gb, ALU.mult).then_inc(S("ygated"), 1)
                if n + 1 < NCH:
                    dve.wait_ge(S(f"y_loaded{n + 1}"), 32)
                    y0 = chunk_of(ych[0], n + 1)
                    dve.tensor_tensor(y0, y0, chunk_of(ych[1], n + 1), ALU.add).then_inc(S("ysum"), 1)
                if n >= 1:
                    dve.wait_ge(S("ygated"), n)
                    xc = chunk_of(xs, n - 1)
                    dve.tensor_tensor(xc, xc, chunk_of(ych[0], n - 1), ALU.add).then_inc(S("out_ready"), 1)


def kernel(L0_attn_x, L0_attn_time_decay, L0_attn_time_first, L0_attn_time_mix_k, L0_attn_time_mix_v,
           L0_attn_time_mix_r, L0_attn_Wk, L0_attn_Wv, L0_attn_Wr, L0_attn_Wo, L0_ffn_gate_w, L0_ffn_w1,
           L0_ffn_w2, L0_ffn_w3, L0_c, L0_wmod):
    import numpy as np
    import concourse.bacc as bacc
    from concourse.bass_utils import run_bass_kernel_spmd

    a = np.asarray
    arrays = {
        "x": a(L0_attn_x),
        "par": np.stack([a(v).reshape(-1) for v in (L0_attn_time_decay, L0_attn_time_first, L0_attn_time_mix_k,
                                                    L0_attn_time_mix_v, L0_attn_time_mix_r)], 1),
        "wproj": np.stack([a(w).T for w in (L0_attn_Wk, L0_attn_Wv, L0_attn_Wr, L0_attn_Wo)], 1),
        "gatew": a(L0_ffn_gate_w).T,
        "w1": a(L0_ffn_w1).transpose(2, 0, 1).reshape(P, E * F),
        "w3": a(L0_ffn_w3).transpose(2, 0, 1).reshape(P, E * F),
        "w2": a(L0_ffn_w2).reshape(E, C, FB, P).transpose(3, 0, 2, 1).reshape(P, E * F),
        "cT": a(L0_c).T,
        "wmod": a(L0_wmod),
    }
    arrays = {k: np.ascontiguousarray(v) for k, v in arrays.items()}
    nc = bacc.Bacc("TRN2", target_bir_lowering=False, num_devices=1)
    aps = [nc.dram_tensor("in_" + k, v.shape, mybir.dt.from_np(v.dtype), kind="ExternalInput").ap()
           for k, v in arrays.items()]
    out = nc.dram_tensor("out", (B, T, C), F32, kind="ExternalOutput").ap()
    block_program(nc, *aps, out)
    r = run_bass_kernel_spmd(nc, [{"in_" + k: v for k, v in arrays.items()}], core_ids=[0])
    return r.results[0]["out"]
```
